# Optimizing a Trainium2 kernel written in Bass

```python
import numpy as np
import jax
import jax.numpy as jnp

def _softmax(x, axis=-1):
    return jax.nn.softmax(x, axis=axis)

def _gelu(x):
    return jax.nn.gelu(x, approximate=True)

def _silu(x):
    return jax.nn.silu(x)

def _sigmoid(x):
    return jax.nn.sigmoid(x)

def _layernorm(x, axis=-1, eps=1e-05):
    m = jnp.mean(x, axis=axis, keepdims=True)
    v = jnp.var(x, axis=axis, keepdims=True)
    return (x - m) / jnp.sqrt(v + eps)

def _scatter_add(tgt, idx, src, axis=0):
    return tgt.at[idx].add(src)

def _segment_sum(src, seg, n):
    return jax.ops.segment_sum(src, seg, n)
kernel_name = 'mk_seq_preln_d2_jaxref_r8_e7e192'

def setup_inputs(seed: int=0):
    np.random.seed(seed)
    _w = jnp.asarray

    def _L0_attn_setup():
        import jax, jax.numpy as jnp
        import numpy as np
        B, S, D, H = (4, 1024, 128, 16)
        HD = D // H

        def elu_feature_map(x):
            return jax.nn.elu(x) + 1.0
        key = jax.random.key(seed)
        k1, k2, k3 = jax.random.split(key, 3)
        x = jax.random.normal(k1, (B, S, D), dtype=jnp.float32)
        w_qkv = jax.random.normal(k2, (3 * D, D), dtype=jnp.float32) * D ** (-0.5)
        w_out = jax.random.normal(k3, (D, D), dtype=jnp.float32) * D ** (-0.5)
        return {'x': x, 'w_qkv': w_qkv, 'w_out': w_out}
    _L0_attn_in = _L0_attn_setup()

    def _L0_ffn_setup():
        import jax, jax.numpy as jnp
        import numpy as np
        B, T, D, FF, E, TOP_K = (8, 256, 128, 512, 8, 2)
        key = jax.random.key(seed)
        kx, kr, k1, k2 = jax.random.split(key, 4)
        x = jax.random.normal(kx, (B, T, D), dtype=jnp.float32)
        Wr = jax.random.normal(kr, (E, D), dtype=jnp.float32) * 0.02
        W1 = jax.random.normal(k1, (E, D, FF), dtype=jnp.float32) * 0.02
        W2 = jax.random.normal(k2, (E, FF, D), dtype=jnp.float32) * 0.02
        return {'x': x, 'Wr': Wr, 'W1': W1, 'W2': W2}
    _L0_ffn_in = _L0_ffn_setup()

    def _L1_attn_setup():
        import jax, jax.numpy as jnp
        import numpy as np
        DIMS = 128
        HEADS = 16
        HEAD_DIM = DIMS // HEADS
        key = jax.random.key(seed)
        k_x, k_q, k_k, k_v = jax.random.split(key, 4)
        scale = 1.0 / np.sqrt(DIMS)
        return {'input_seq_embs': jax.random.normal(k_x, (4, 512, DIMS), dtype=jnp.float32), 'W_Q': jax.random.normal(k_q, (DIMS, DIMS), dtype=jnp.float32) * scale, 'W_K': jax.random.normal(k_k, (DIMS, DIMS), dtype=jnp.float32) * scale, 'W_V': jax.random.normal(k_v, (DIMS, DIMS), dtype=jnp.float32) * scale}
    _L1_attn_in = _L1_attn_setup()

    def _L1_ffn_setup():
        import jax, jax.numpy as jnp
        import numpy as np
        DIM = 128

        def _reference_tuple_inner(x, W_r, W_k, W_v, mu_r, mu_k):
            B, T, C = x.shape
            x_prev = jnp.concatenate([jnp.zeros((B, 1, C), x.dtype), x[:, :-1, :]], axis=1)
            xr = mu_r * x + (1.0 - mu_r) * x_prev
            xk = mu_k * x + (1.0 - mu_k) * x_prev
            r = jax.nn.sigmoid(jnp.einsum('btc,dc->btd', xr, W_r))
            k = jnp.einsum('btc,dc->btd', xk, W_k)
            k_act = jnp.square(jax.nn.relu(k))
            out = r * jnp.einsum('btc,dc->btd', k_act, W_v)
            new_state = x[:, -1, :]
            return (out, new_state)
        key = jax.random.key(seed)
        ks = jax.random.split(key, 6)
        B, T, C = (8, 256, DIM)
        x = jax.random.normal(ks[0], (B, T, C), dtype=jnp.float32)
        s = 1.0 / np.sqrt(C)
        W_r = jax.random.uniform(ks[1], (C, C), jnp.float32, -s, s)
        W_k = jax.random.uniform(ks[2], (C, C), jnp.float32, -s, s)
        W_v = jax.random.uniform(ks[3], (C, C), jnp.float32, -s, s)
        mu_r = jax.random.uniform(ks[4], (C,), jnp.float32)
        mu_k = jax.random.uniform(ks[5], (C,), jnp.float32)
        return {'x': x, 'W_r': W_r, 'W_k': W_k, 'W_v': W_v, 'mu_r': mu_r, 'mu_k': mu_k}
    _L1_ffn_in = _L1_ffn_setup()
    _d = {'L0_attn_x': _L0_attn_in['x'], 'L0_attn_w_qkv': _L0_attn_in['w_qkv'], 'L0_attn_w_out': _L0_attn_in['w_out'], 'L0_ffn_Wr': _L0_ffn_in['Wr'], 'L0_ffn_W1': _L0_ffn_in['W1'], 'L0_ffn_W2': _L0_ffn_in['W2'], 'L1_attn_W_Q': _L1_attn_in['W_Q'], 'L1_attn_W_K': _L1_attn_in['W_K'], 'L1_attn_W_V': _L1_attn_in['W_V'], 'L1_ffn_W_r': _L1_ffn_in['W_r'], 'L1_ffn_W_k': _L1_ffn_in['W_k'], 'L1_ffn_W_v': _L1_ffn_in['W_v'], 'L1_ffn_mu_r': _L1_ffn_in['mu_r'], 'L1_ffn_mu_k': _L1_ffn_in['mu_k']}
    _x0 = _d['L0_attn_x']
    _d['L0_attn_x'] = jax.random.normal(jax.random.fold_in(jax.random.key(seed), 1), (16, 256, 128), dtype=_x0.dtype)
    del _x0
    return _d

def reference(L0_attn_x, L0_attn_w_qkv, L0_attn_w_out, L0_ffn_Wr, L0_ffn_W1, L0_ffn_W2, L1_attn_W_Q, L1_attn_W_K, L1_attn_W_V, L1_ffn_W_r, L1_ffn_W_k, L1_ffn_W_v, L1_ffn_mu_r, L1_ffn_mu_k):

    def _L0_attn_ref(x, w_qkv, w_out):
        import jax, jax.numpy as jnp
        import numpy as np
        B, S, D, H = (4, 1024, 128, 16)
        HD = D // H

        def elu_feature_map(x):
            return jax.nn.elu(x) + 1.0
        Bv, Sv, Dv = x.shape
        qkv = (x @ w_qkv.T).reshape(Bv, Sv, 3, H, HD)
        qkv = jnp.transpose(qkv, (2, 0, 3, 1, 4))
        q, k, v = (qkv[0], qkv[1], qkv[2])
        q = elu_feature_map(q)
        k = elu_feature_map(k)
        kv = jnp.einsum('bhsd,bhse->bhde', k, v)
        out = jnp.einsum('bhsd,bhde->bhse', q, kv)
        k_sum = k.sum(axis=2)
        normalizer = jnp.einsum('bhsd,bhd->bhs', q, k_sum)[..., None]
        normalizer = jnp.maximum(normalizer, 1e-06)
        out = (out / normalizer).transpose(0, 2, 1, 3).reshape(Bv, Sv, Dv)
        return out @ w_out.T

    def _L0_ffn_ref(x, Wr, W1, W2):
        import jax, jax.numpy as jnp
        import numpy as np
        B, T, D, FF, E, TOP_K = (8, 256, 128, 512, 8, 2)
        Bs, Ts, Ds = x.shape
        Ne = Wr.shape[0]
        xf = x.reshape(-1, Ds)
        N = xf.shape[0]
        logits = xf @ Wr.T
        topk_vals, topk_idx = jax.lax.top_k(logits, TOP_K)
        w = jax.nn.softmax(topk_vals.astype(jnp.float32), axis=-1).astype(x.dtype)
        idx_flat = topk_idx.reshape(-1)
        w_flat = w.reshape(-1)
        sort_idx = jnp.argsort(idx_flat)
        rev = sort_idx // TOP_K
        sw = w_flat[sort_idx]
        perm = xf[rev]
        S = perm.shape[0]
        chunks = perm.reshape(Ne, S // Ne, Ds)
        h = jax.nn.gelu(jnp.einsum('ecd,edf->ecf', chunks, W1), approximate=False)
        eo = jnp.einsum('ecf,efd->ecd', h, W2).reshape(S, Ds)
        out = jnp.zeros((N, Ds), dtype=x.dtype).at[rev].add(eo * sw[:, None])
        return out.reshape(Bs, Ts, Ds)

    def _L1_attn_ref(input_seq_embs, W_Q, W_K, W_V):
        import jax, jax.numpy as jnp
        import numpy as np
        DIMS = 128
        HEADS = 16
        HEAD_DIM = DIMS // HEADS
        B, L, d = input_seq_embs.shape
        H, hd = (HEADS, HEAD_DIM)
        Q = (input_seq_embs @ W_Q.T).reshape(B, L, H, hd)
        K = (input_seq_embs @ W_K.T).reshape(B, L, H, hd)
        V = (input_seq_embs @ W_V.T).reshape(B, L, H, hd)
        sK = jax.nn.softmax(jnp.swapaxes(K, -1, -2), axis=-1)
        tran_V = jnp.einsum('bldh,blhe->blde', sK, V)
        out = jnp.einsum('blhd,blde->blhe', jax.nn.softmax(Q, axis=-1), tran_V)
        return out.reshape(B, L, d)

    def _L1_ffn_ref(x, W_r, W_k, W_v, mu_r, mu_k):
        import jax, jax.numpy as jnp
        import numpy as np
        DIM = 128

        def _reference_tuple_inner(x, W_r, W_k, W_v, mu_r, mu_k):
            B, T, C = x.shape
            x_prev = jnp.concatenate([jnp.zeros((B, 1, C), x.dtype), x[:, :-1, :]], axis=1)
            xr = mu_r * x + (1.0 - mu_r) * x_prev
            xk = mu_k * x + (1.0 - mu_k) * x_prev
            r = jax.nn.sigmoid(jnp.einsum('btc,dc->btd', xr, W_r))
            k = jnp.einsum('btc,dc->btd', xk, W_k)
            k_act = jnp.square(jax.nn.relu(k))
            out = r * jnp.einsum('btc,dc->btd', k_act, W_v)
            new_state = x[:, -1, :]
            return (out, new_state)
        return _reference_tuple_inner(x, W_r, W_k, W_v, mu_r, mu_k)[0]
    x = L0_attn_x
    x = x + _L0_attn_ref(_layernorm(x, axis=-1), L0_attn_w_qkv, L0_attn_w_out)
    x = x + _L0_ffn_ref(_layernorm(x, axis=-1), L0_ffn_Wr, L0_ffn_W1, L0_ffn_W2)
    x = x + _L1_attn_ref(_layernorm(x, axis=-1), L1_attn_W_Q, L1_attn_W_K, L1_attn_W_V)
    x = x + _L1_ffn_ref(_layernorm(x, axis=-1), L1_ffn_W_r, L1_ffn_W_k, L1_ffn_W_v, L1_ffn_mu_r, L1_ffn_mu_k)
    return x

_drawn_inputs = setup_inputs


def setup_inputs(seed=0):
    import zlib

    import numpy as np

    out = dict(_drawn_inputs(seed))
    spreads = {}
    factors = {'L1_ffn_W_r': 3.29, 'L1_ffn_mu_r': 6.469}
    for name, (base, spread) in spreads.items():
        noise = np.random.default_rng([zlib.crc32(name.encode()), seed]).standard_normal(out[name].shape)
        drawn = base * np.exp(spread * noise) if base else spread * noise
        out[name] = jnp.asarray(drawn.astype(out[name].dtype))
    for name, factor in factors.items():
        out[name] = (out[name] * factor).astype(out[name].dtype)
    return out
```

```python
from collections import namedtuple
from contextlib import ExitStack

import concourse.bass as bass
from concourse import mybir

F32 = mybir.dt.float32
BF16 = mybir.dt.bfloat16
U32 = mybir.dt.uint32
ALU = mybir.AluOpType
ACT = mybir.ActivationFunctionType
AX = mybir.AxisListType

P = 128
D = 128
HEADS = 16
HD = D // HEADS
EPS = 1e-5

Slot = namedtuple("Slot", "m k unroll steady count")
Step = namedtuple("Step", "t pair quad k steady")


def run_slots(eng, count, last_lag, unroll, body):
    peeled = -(-(last_lag + 2) // unroll)
    for m in range(peeled):
        for k in range(unroll):
            body(Slot(m, k, unroll, False, count))
    with eng.Fori(peeled, count // unroll) as m:
        for k in range(unroll):
            body(Slot(m, k, unroll, True, count))
    for s in range(count, count + last_lag):
        body(Slot(s // unroll, s % unroll, unroll, False, count))


def item(slot, lag):
    j = slot.k - lag
    t = slot.unroll * slot.m + j
    if not slot.steady and not 0 <= t < slot.count:
        return None
    return Step(t, (slot.unroll // 2) * slot.m + j // 2, slot.m + j // 4, j % slot.unroll, slot.steady)


def has_prior(st, n):
    return st.steady or st.t >= n


def build(nc, x, wa, w1, w2, mu, out):
    B, T = 16, 256
    TPB = T // P
    N = B * T
    NT = N // P
    E, FF = w1.shape[0], w1.shape[2]
    FB = FF // P
    K = 2
    NS = N * K // P
    G = 4
    NG = NS // G
    GPC = NG // E
    assert GPC == 2 and TPB == 2

    cQ, cKV, cO, cR = 0, D, 3 * D, 4 * D
    cQKV = cR + E
    cFR = cQKV + 3 * D
    cFK, cFV = cFR + D, cFR + 2 * D
    cEnd = cFR + 3 * D
    assert wa.shape == (P, cEnd)

    xn_dram = nc.dram_tensor("xn_dram", (P * NT, D), F32).ap()
    eo_dram = nc.dram_tensor("eo_dram", (P * NS, D), F32).ap()
    xn_rows = xn_dram.rearrange("(p t) d -> p t d", p=P)
    eo_rows = eo_dram.rearrange("(p t) d -> p t d", p=P)

    with ExitStack() as ctx:
        def sb(name, shape, dt=F32):
            return ctx.enter_context(nc.sbuf_tensor(name, shape, dt))

        def two(name, shape, dt=F32):
            return [sb(f"{name}{i}", shape, dt) for i in range(2)]

        def sem(name):
            return ctx.enter_context(nc.semaphore(name))

        psum = ctx.enter_context(nc.psum_tensor("psum", [P, 8, 512], F32))
        bank = [psum[:, i, :] for i in range(8)]

        W = sb("W", [P, cEnd])
        MU = sb("MU", [P, 2])
        ident = sb("ident", [P, P])
        block_mask = sb("block_mask", [P, D + HEADS])
        neg_half = sb("neg_half", [P, TPB])
        iota_e = sb("iota_e", [P, E])
        before = sb("before", [P, P], BF16)
        ones = sb("ones", [P, P], BF16)
        iota_lo = sb("iota_lo", [P, P])
        iota_part = sb("iota_part", [P, 1])
        iota_tile = sb("iota_tile", [P, NT])

        X = sb("X", [P, NT, D])
        TOPV = sb("TOPV", [P, NT, K])
        TOPI = sb("TOPI", [P, NT, K])

        stats = two("stats", [P, TPB, 6])
        mv = two("mv", [P, TPB, 2])
        rstd = two("rstd", [P, TPB])
        veps = two("veps", [P, TPB])
        stats2 = two("stats2", [P, TPB, 6])
        mv2 = two("mv2", [P, TPB, 2])
        rstd2 = two("rstd2", [P, TPB])
        veps2 = two("veps2", [P, TPB])
        xn = two("xn", [P, TPB, D])
        xnT = two("xnT", [P, T])
        eq = two("eq", [P, T + TPB * D])
        em = two("em", [P, T + TPB * D])
        qT = two("qT", [P, T])
        kt = two("kt", [P, TPB, D])
        vt = two("vt", [P, TPB, D + 1])
        kv = two("kv", [P, D + HEADS])
        den = two("den", [P, TPB, HEADS])
        rden = two("rden", [P, TPB, HEADS])
        att = two("att", [P, TPB, D])
        attT = two("attT", [P, T])
        xm = two("xm", [P, TPB, D])
        xmT = two("xmT", [P, T])
        lg = two("lg", [P, TPB, E])
        top8 = two("top8", [P, TPB, 8])
        idx8 = two("idx8", [P, TPB, 8], U32)

        OH = sb("OH", [P, K, E, NT])
        CNT = sb("CNT", [P, E, NT], BF16)
        CNTf = sb("CNTf", [P, E * NT])
        ONEf = sb("ONEf", [P, E * NT])
        TOT = sb("TOT", [P, E * NT])
        CUM = sb("CUM", [P, E * NT])
        BASE = sb("BASE", [P, E * NT])
        PRD = sb("PRD", [P, K, E, NT])
        POSf = sb("POSf", [P, K, NT])
        POSu = sb("POSu", [P, K * NT], U32)
        LOu = sb("LOu", [P, K * NT], U32)
        HIu = sb("HIu", [P, K * NT], U32)
        LOf = sb("LOf", [P, K * NT])
        HIf = sb("HIf", [P, K * NT])
        EIDX = sb("EIDX", [P, K * NT], U32)
        OHLO = sb("OHLO", [P, K * NT, P], BF16)
        OHHI = sb("OHHI", [P, K * NT, 2 * NS], BF16)
        SIDXf = sb("SIDXf", [P, NS])
        SIDX = sb("SIDX", [P, NS], U32)
        GD = sb("GD", [P, NT])
        GE = sb("GE", [P, NT])
        GS = sb("GS", [P, NT])
        GW = sb("GW", [P, K, NT])

        W1s = two("W1s", [P, FF])
        W2s = two("W2s", [P, FB, D])
        xg = two("xg", [P, G, D])
        xgT = two("xgT", [P, G * P])
        h = two("h", [P, FB, G * P])
        eo = two("eo", [P, G, D])

        ge = [sb(f"ge{i}", [P, TPB * K, D]) for i in range(2)]
        xs = two("xs", [P, TPB, D])
        x2 = [sb(f"x2_{i}", [P, TPB, D]) for i in range(4)]
        y3 = two("y3", [P, TPB, D])
        y3T = two("y3T", [P, T])
        qmax = two("qmax", [P, TPB, HEADS])
        kmax = two("kmax", [P, TPB, HD])
        qk = two("qk", [P, TPB, 2 * D])
        qke = two("qke", [P, TPB, 2 * D])
        vc = two("vc", [P, TPB, D])
        qsum = two("qsum", [P, TPB, HEADS])
        ksum = two("ksum", [P, TPB, HD])
        rqs = two("rqs", [P, TPB, HEADS])
        rks = two("rks", [P, TPB, HD])
        p1 = two("p1", [P, HEADS * HD * HD])
        tv = two("tv", [P, TPB, HD * HD])
        p2 = two("p2", [P, HD * HEADS * HD])
        ao = two("ao", [P, TPB, D])
        x3 = [sb(f"x3_{i}", [P, TPB, D]) for i in range(4)]
        y4 = two("y4", [P, TPB, D])
        y4T = two("y4T", [P, 1 + T])
        dx = two("dx", [P, T])
        xr = two("xr", [P, T])
        xk = two("xk", [P, T])
        kr = two("kr", [P, T])
        ka = two("ka", [P, T])
        th = two("th", [P, TPB, D])
        rkv = two("rkv", [P, TPB, D])
        fin = two("fin", [P, TPB, D])

        SIDX_col = two("SIDX_col", [P, G], U32)
        EIDX_col = two("EIDX_col", [P, TPB * K], U32)

        idx_copied = sem("idx_copied")
        eidx_copied = sem("eidx_copied")
        weights_in = sem("weights_in")
        consts_made = sem("consts_made")
        x_in = [sem(f"x_in{i}") for i in range(2)]
        names = """a_stats a_mv a_veps a_rstd a_xn a_xnT_ps a_xnT a_proj a_eq a_v a_em a_elu a_kv_ps a_kv
            a_num a_den a_rden a_att a_attT_ps a_attT a_wo a_x1 b_stats b_mv b_veps b_rstd b_xm b_xmT_ps b_xmT
            b_logits b_lg b_top8 b_idx8 b_topv b_top
            a_mv_1 a_xn_1 b_mv_1 b_xm_1 a_kv0 a_att_1 a_eq0 a_elu0""".split()
        S = {n: sem(n) for n in names}
        xn_stored = [sem(f"xn_stored{i}") for i in range(2)]
        routed = sem("routed")
        counts_ps = sem("counts_ps")
        gates_diff = sem("gates_diff")
        gates_exp = sem("gates_exp")
        oh_made = sem("oh_made")
        counts_made = sem("counts_made")
        onehots = sem("onehots")
        ids_ps = sem("ids_ps")
        ids_ready = sem("ids_ready")
        w_in = [sem(f"w_in{i}") for i in range(2)]
        names = "f_xgT_ps f_xgT f_h_ps f_h f_out_ps f_eo".split()
        F = {n: sem(n) for n in names}
        xg_in = [sem(f"xg_in{i}") for i in range(2)]
        eo_stored = [sem(f"eo_stored{i}") for i in range(2)]
        ge_in = [sem(f"ge_in{i}") for i in range(2)]
        names = """c_half c_x2 c_stats c_mv c_veps c_rstd c_y3 c_y3T_ps c_y3T c_proj c_qmax c_kmax c_qk0 c_qk c_qke
            c_v c_ksum c_rks c_qsum c_rqs c_p1 c_tv_ps c_tv c_p2 c_out_ps c_ao c_x3 d_stats d_mv d_veps d_rstd d_y4 d_y4T_ps
            d_y4T d_dx d_mix d_rk_ps d_relu d_th d_ka d_v_ps d_rkv d_fin
            c_mv_1 c_x2_1 c_y3_1 d_mv_1 d_y4_1 d_mix0 c_heads""".split()
        C = {n: sem(n) for n in names}
        out_stored = [sem(f"out_stored{i}") for i in range(2)]
        zeroed = sem("zeroed")

        consts = 20

        def wait_alone(eng, sem_, value):
            value = value if isinstance(value, int) else eng.to_reg(value)
            eng.wait_ge(consts_made, consts)
            eng.wait_ge(sem_, value)

        block = ctx.enter_context(nc.Block())

        @block.sync
        def _(sp):
            sp.dma_start(W[:], wa).then_inc(weights_in, 16)
            sp.dma_start(MU[:], mu).then_inc(weights_in, 16)

            def slot_a(s):
                if st := item(s, 0):
                    if has_prior(st, 2):
                        wait_alone(sp, x_in[st.k % 2], 16 * st.pair)
                    sp.dma_start(X[:, bass.ts(st.t, TPB), :], x[:, bass.ts(st.t, TPB), :])\
                        .then_inc(x_in[st.k % 2], 16)
                if st := item(s, 4):
                    if has_prior(st, 2):
                        wait_alone(sp, xn_stored[st.k % 2], 16 * st.pair)
                    wait_alone(sp, S["b_xm"], st.t + 1)
                    sp.dma_start(xn_rows[:, bass.ts(st.t, TPB), :], xm[st.k % 2][:])\
                        .then_inc(xn_stored[st.k % 2], 16)

            run_slots(sp, B, 4, 2, slot_a)

            def slot_b(s):
                st = item(s, 0)
                if st and st.k % 2 == 0:
                    half = (st.k // 2) % 2
                    if has_prior(st, 4):
                        wait_alone(sp, F["f_out_ps"], st.t - 2)
                    sp.dma_start(W1s[half][:], w1[st.pair]).then_inc(w_in[half], 16)
                    sp.dma_start(W2s[half][:], w2[st.pair]).then_inc(w_in[half], 16)
                if st := item(s, 2):
                    if has_prior(st, 2):
                        wait_alone(sp, eo_stored[st.k % 2], 16 * st.pair)
                    wait_alone(sp, F["f_eo"], st.t + 1)
                    sp.dma_start(eo_rows[:, bass.ts(st.t, G), :], eo[st.k % 2][:])\
                        .then_inc(eo_stored[st.k % 2], 16)

            run_slots(sp, NG, 2, 4, slot_b)

            def slot_c(s):
                if st := item(s, 0):
                    if has_prior(st, 2):
                        wait_alone(sp, out_stored[st.k % 2], 16 * st.pair)
                    wait_alone(sp, C["d_fin"], st.t + 1)
                    sp.dma_start(out[:, bass.ts(st.t, TPB), :], fin[st.k % 2][:])\
                        .then_inc(out_stored[st.k % 2], 16)

            run_slots(sp, B, 0, 2, slot_c)
            for s in out_stored:
                sp.wait_ge(s, 16 * B // 2)

        @block.gpsimd
        def _(pool):
            pool.memset(ident[:], 0.0).then_inc(consts_made, 1)
            pool.memset(block_mask[:], 1.0).then_inc(consts_made, 1)
            pool.memset(before[:], 1.0).then_inc(consts_made, 1)
            pool.memset(ones[:], 1.0).then_inc(consts_made, 1)
            pool.memset(ONEf[:], 1.0).then_inc(consts_made, 1)
            pool.memset(neg_half[:], -0.5).then_inc(consts_made, 1)
            for v in vt:
                pool.memset(v[:, :, D:D + 1], 1.0).then_inc(consts_made, 1)
            for y in y4T:
                pool.memset(y[:, 0:1], 0.0).then_inc(consts_made, 1)
            pool.iota(iota_e[:], [[1, E]], base=0, channel_multiplier=0,
                      allow_small_or_imprecise_dtypes=True).then_inc(consts_made, 1)
            pool.iota(iota_lo[:], [[1, P]], base=0, channel_multiplier=0,
                      allow_small_or_imprecise_dtypes=True).then_inc(consts_made, 1)
            pool.iota(iota_part[:], [[0, 1]], base=0, channel_multiplier=1,
                      allow_small_or_imprecise_dtypes=True).then_inc(consts_made, 1)
            pool.iota(iota_tile[:], [[1, NT]], base=0, channel_multiplier=0,
                      allow_small_or_imprecise_dtypes=True).then_inc(consts_made, 1)
            pool.wait_ge(consts_made, 14)
            pool.affine_select(out=ident[:], in_=ident[:], compare_op=ALU.not_equal, fill=1.0, base=0,
                               pattern=[[-1, P]], channel_multiplier=1).then_inc(consts_made, 1)
            pool.affine_select(out=before[:], in_=before[:], compare_op=ALU.is_gt, fill=0.0, base=0,
                               pattern=[[1, P]], channel_multiplier=-1).then_inc(consts_made, 1)
            by_head = block_mask[:, 0:D].rearrange("p (h j) -> p h j", j=HD)
            heads = block_mask[:, D:D + HEADS]
            pool.affine_select(out=by_head, in_=by_head, compare_op=ALU.is_ge, fill=0.0, base=0,
                               pattern=[[-HD, HEADS], [0, HD]], channel_multiplier=1).then_inc(consts_made, 1)
            pool.affine_select(out=heads, in_=heads, compare_op=ALU.is_ge, fill=0.0, base=0,
                               pattern=[[-HD, HEADS]], channel_multiplier=1).then_inc(consts_made, 1)
            pool.wait_ge(consts_made, 18)
            pool.affine_select(out=by_head, in_=by_head, compare_op=ALU.is_ge, fill=0.0, base=HD - 1,
                               pattern=[[HD, HEADS], [0, HD]], channel_multiplier=-1).then_inc(consts_made, 1)
            pool.affine_select(out=heads, in_=heads, compare_op=ALU.is_ge, fill=0.0, base=HD - 1,
                               pattern=[[HD, HEADS]], channel_multiplier=-1).then_inc(consts_made, 1)
            pool.wait_ge(consts_made, consts)

            def rsqrt(st, sems, ready, added, done, mv_, veps_, rstd_):
                i = st.k % 2
                wait_alone(pool, sems[ready], st.t + 1)
                pool.tensor_scalar(veps_[i][:], mv_[i][:, :, 1], EPS, None, ALU.add).then_inc(sems[added], 1)
                pool.wait_ge(sems[added], st.t + 1)
                pool.tensor_tensor(rstd_[i][:], veps_[i][:], neg_half[:], ALU.pow).then_inc(sems[done], 1)

            def slot_a(s):
                if st := item(s, 0):
                    rsqrt(st, S, "a_mv", "a_veps", "a_rstd", mv, veps, rstd)
                if st := item(s, 3):
                    rsqrt(st, S, "b_mv", "b_veps", "b_rstd", mv2, veps2, rstd2)
                if st := item(s, 1):
                    i = st.k % 2
                    wait_alone(pool, S["a_eq"], st.t + 1)
                    if has_prior(st, 2):
                        pool.wait_ge(S["a_elu"], st.t - 1)
                    pool.tensor_scalar(em[i][:], eq[i][:], 1.0, None, ALU.min).then_inc(S["a_em"], 1)

            run_slots(pool, B, 4, 2, slot_a)

            pool.wait_ge(ids_ready, 1)
            for s in xn_stored:
                pool.wait_ge(s, 16 * B // 2)

            def slot_b(s):
                if st := item(s, 0):
                    i = st.k % 2
                    if has_prior(st, 2):
                        pool.wait_ge(F["f_xgT_ps"], st.t - 1)
                        pool.wait_ge(xg_in[i], 16 * G * st.pair)
                    pool.tensor_copy(SIDX_col[i][:], SIDX[:, bass.ts(st.t, G)]).then_inc(idx_copied, 1)
                    wait_alone(pool, idx_copied, st.t + 1)
                    for j in range(G):
                        pool.indirect_dma_start(
                            xg[i][:, j, :], None, xn_dram,
                            bass.IndirectOffsetOnAxis(ap=SIDX_col[i][:, j:j + 1], axis=0)).then_inc(xg_in[i], 16)

            run_slots(pool, NG, 0, 4, slot_b)
            for s in eo_stored:
                pool.wait_ge(s, 16 * NG // 2)

            def slot_c(s):
                if st := item(s, 0):
                    i = st.k % 2
                    if has_prior(st, 2):
                        pool.wait_ge(C["c_x2"], st.t - 1)
                        pool.wait_ge(ge_in[i], 16 * G * st.pair)
                    for c in range(K):
                        pool.tensor_copy(EIDX_col[i][:, c * TPB:(c + 1) * TPB],
                                         EIDX[:, bass.ds(st.t * TPB + c * NT, TPB)]).then_inc(eidx_copied, 1)
                    wait_alone(pool, eidx_copied, 2 * st.t + 2)
                    for j in range(TPB * K):
                        pool.indirect_dma_start(
                            ge[i][:, j, :], None, eo_dram,
                            bass.IndirectOffsetOnAxis(ap=EIDX_col[i][:, j:j + 1], axis=0)).then_inc(ge_in[i], 16)
                if st := item(s, 1):
                    rsqrt(st, C, "c_mv", "c_veps", "c_rstd", mv, veps, rstd)
                if st := item(s, 4):
                    rsqrt(st, C, "d_mv", "d_veps", "d_rstd", mv2, veps2, rstd2)

            run_slots(pool, B, 6, 2, slot_c)

        @block.scalar
        def _(act):
            def evacuate(st, sems, ready, done, dst, src):
                act.wait_ge(sems[ready], st.t + 1)
                act.activation(dst, src, ACT.Copy).then_inc(sems[done], 1)

            def slot_a(s):
                if st := item(s, 1):
                    evacuate(st, S, "a_xnT_ps", "a_xnT", xnT[st.k % 2][:], bank[0][:, 0:T])
                if st := item(s, 4):
                    evacuate(st, S, "b_xmT_ps", "b_xmT", xmT[st.k % 2][:], bank[7][:, 0:T])
                if st := item(s, 2):
                    evacuate(st, S, "a_attT_ps", "a_attT", attT[st.k % 2][:], bank[5][:, 0:T])
                if st := item(s, 1):
                    i = st.k % 2
                    act.wait_ge(S["a_proj"], st.t + 1)
                    if has_prior(st, 2):
                        act.wait_ge(S["a_em"], st.t - 1)
                    kvp = bank[2].rearrange("p (n w d) -> p n w d", n=TPB, w=2)
                    act.activation(eq[i][:, 0:T], bank[1][:, 0:T], ACT.Exp).then_inc(S["a_eq0"], 1)
                    act.activation(eq[i][:, T:].rearrange("p (n d) -> p n d", n=TPB), kvp[:, :, 0, :],
                                   ACT.Exp).then_inc(S["a_eq"], 1)
                    act.activation(vt[i][:, :, 0:D], kvp[:, :, 1, :], ACT.Copy).then_inc(S["a_v"], 1)

            run_slots(act, B, 4, 2, slot_a)

            act.wait_ge(gates_diff, 1)
            act.activation(GE[:], GD[:], ACT.Exp).then_inc(gates_exp, 1)

            def slot_b(s):
                if st := item(s, 1):
                    i = st.k % 2
                    for f in range(FB):
                        act.wait_ge(F["f_h_ps"], FB * st.t + f + 1)
                        act.activation(h[i][:, f, :], bank[2 + f], ACT.Gelu).then_inc(F["f_h"], 1)

            run_slots(act, NG, 1, 4, slot_b)

            def slot_c(s):
                if st := item(s, 2):
                    evacuate(st, C, "c_y3T_ps", "c_y3T", y3T[st.k % 2][:], bank[0][:, 0:T])
                if st := item(s, 5):
                    evacuate(st, C, "d_y4T_ps", "d_y4T", y4T[st.k % 2][:, 1:], bank[0][:, T:2 * T])
                if st := item(s, 6):
                    i = st.k % 2
                    act.wait_ge(C["d_rk_ps"], st.t + 1)
                    act.activation(kr[i][:], bank[5][:, 0:T], ACT.Relu).then_inc(C["d_relu"], 1)
                    act.activation(th[i][:], bank[6][:, 0:TPB * D].rearrange("p (n d) -> p n d", n=TPB),
                                   ACT.Tanh, scale=0.5).then_inc(C["d_th"], 1)
                    act.wait_ge(C["d_relu"], st.t + 1)
                    act.activation(ka[i][:], kr[i][:], ACT.Square).then_inc(C["d_ka"], 1)
                if st := item(s, 2):
                    i = st.k % 2
                    act.wait_ge(C["c_qk"], st.t + 1)
                    if has_prior(st, 2):
                        act.wait_ge(C["c_p2"], TPB * st.t - TPB)
                    act.activation(vc[i][:], psum[:, 1:3, 2 * D:3 * D], ACT.Copy).then_inc(C["c_v"], 1)
                    act.activation(qke[i][:], qk[i][:], ACT.Exp).then_inc(C["c_qke"], 1)

            run_slots(act, B, 6, 2, slot_c)

        @block.vector
        def _(dve):
            def norm_stats(st, sems, names, rows, stats_, mv_):
                i = st.k % 2
                for n in range(TPB):
                    dve.bn_stats(stats_[i][:, n, :], rows(n)).then_inc(sems[names[0]], 1)
                wait_alone(dve, sems[names[0]], TPB * st.t + TPB)
                for n in range(TPB):
                    dve.bn_aggr(mv_[i][:, n, :], stats_[i][:, n, :]).then_inc(sems[names[1] + "_1" * (n == 0)], 1)

            def norm_apply(st, sems, ready, done, rows, mv_, rstd_, dst):
                i = st.k % 2
                dve.wait_ge(sems[ready], st.t + 1)
                for n in range(TPB):
                    dve.tensor_scalar(dst[i][:, n, :], rows(n), mv_[i][:, n, 0:1], rstd_[i][:, n:n + 1],
                                      ALU.subtract, ALU.mult).then_inc(sems[done + "_1" * (n == 0)], 1)

            dve.wait_ge(consts_made, consts)

            def slot_a(s):
                if st := item(s, 2):
                    i = st.k % 2
                    dve.wait_ge(S["a_kv_ps"], st.t + 1)
                    if has_prior(st, 2):
                        dve.wait_ge(S["a_num"], st.t - 1)
                    dve.tensor_tensor(kv[i][:, 0:D], bank[3][:, 0:D], block_mask[:, 0:D], ALU.mult)\
                        .then_inc(S["a_kv0"], 1)
                    dve.tensor_scalar(kv[i][:, D:], block_mask[:, D:], bank[3][:, D:D + 1], None, ALU.mult)\
                        .then_inc(S["a_kv"], 1)
                if st := item(s, 0):
                    wait_alone(dve, x_in[st.k % 2], 16 * (st.pair + 1))
                    norm_stats(st, S, ("a_stats", "a_mv"), lambda n: X[:, st.t * TPB + n, :], stats, mv)
                if st := item(s, 3):
                    dve.wait_ge(S["a_wo"], st.t + 1)
                    rows = X[:, bass.ts(st.t, TPB), :]
                    dve.tensor_tensor(rows, bank[6][:, 0:TPB * D].rearrange("p (n d) -> p n d", n=TPB),
                                      rows, ALU.add).then_inc(S["a_x1"], 1)
                    wait_alone(dve, S["a_x1"], st.t + 1)
                    norm_stats(st, S, ("b_stats", "b_mv"), lambda n: X[:, st.t * TPB + n, :], stats2, mv2)
                if st := item(s, 0):
                    if has_prior(st, 2):
                        dve.wait_ge(S["a_xnT_ps"], st.t - 1)
                    norm_apply(st, S, "a_rstd", "a_xn", lambda n: X[:, st.t * TPB + n, :], mv, rstd, xn)
                if st := item(s, 2):
                    i = st.k % 2
                    nd = bank[4][:, 0:TPB * (D + HEADS)].rearrange("p (n c) -> p n c", n=TPB)
                    dve.wait_ge(S["a_num"], st.t + 1)
                    dve.tensor_scalar(den[i][:], nd[:, :, D:], 1e-6, None, ALU.max).then_inc(S["a_den"], 1)
                    dve.wait_ge(S["a_den"], st.t + 1)
                    dve.reciprocal(rden[i][:], den[i][:]).then_inc(S["a_rden"], 1)
                    dve.wait_ge(S["a_rden"], st.t + 1)
                    if has_prior(st, 2):
                        dve.wait_ge(S["a_attT_ps"], st.t - 1)
                    for n in range(TPB):
                        dve.tensor_tensor(
                            att[i][:, n, :].rearrange("p (h j) -> p h j", j=HD),
                            nd[:, n, 0:D].rearrange("p (h j) -> p h j", j=HD),
                            rden[i][:, n, :].unsqueeze(2).to_broadcast([P, HEADS, HD]),
                            ALU.mult).then_inc(S["a_att" + "_1" * (n == 0)], 1)
                if st := item(s, 1):
                    i = st.k % 2
                    dve.wait_ge(S["a_em"], st.t + 1)
                    dve.wait_ge(S["a_v"], st.t + 1)
                    if has_prior(st, 2):
                        dve.wait_ge(S["a_num"], st.t - 1)
                    kvp = bank[2].rearrange("p (n w d) -> p n w d", n=TPB, w=2)
                    dve.scalar_tensor_tensor(qT[i][:], bank[1][:, 0:T], 1.0, em[i][:, 0:T], ALU.add, ALU.max)\
                        .then_inc(S["a_elu0"], 1)
                    dve.scalar_tensor_tensor(kt[i][:], kvp[:, :, 0, :], 1.0,
                                             em[i][:, T:].rearrange("p (n d) -> p n d", n=TPB),
                                             ALU.add, ALU.max).then_inc(S["a_elu"], 1)
                if st := item(s, 3):
                    if has_prior(st, 2):
                        dve.wait_ge(S["b_xmT_ps"], st.t - 1)
                        dve.wait_ge(xn_stored[st.k % 2], 16 * st.pair)
                    norm_apply(st, S, "b_rstd", "b_xm", lambda n: X[:, st.t * TPB + n, :], mv2, rstd2, xm)
                if st := item(s, 4):
                    i = st.k % 2
                    dve.wait_ge(S["b_logits"], st.t + 1)
                    dve.tensor_copy(lg[i][:], bank[7][:, 0:TPB * E].rearrange("p (n e) -> p n e", n=TPB))\
                        .then_inc(S["b_lg"], 1)
                    wait_alone(dve, S["b_lg"], st.t + 1)
                    for n in range(TPB):
                        dve.max(top8[i][:, n, :], lg[i][:, n, :]).then_inc(S["b_top8"], 1)
                    wait_alone(dve, S["b_top8"], TPB * st.t + TPB)
                    for n in range(TPB):
                        dve.max_index(idx8[i][:, n, :], top8[i][:, n, :], lg[i][:, n, :]).then_inc(S["b_idx8"], 1)
                    dve.wait_ge(S["b_idx8"], TPB * st.t + TPB)
                    dve.tensor_copy(TOPV[:, bass.ts(st.t, TPB), :], top8[i][:, :, 0:K]).then_inc(S["b_topv"], 1)
                    dve.tensor_copy(TOPI[:, bass.ts(st.t, TPB), :], idx8[i][:, :, 0:K]).then_inc(S["b_top"], 1)

            run_slots(dve, B, 4, 2, slot_a)

            done = 0

            def chain(ins):
                nonlocal done
                done += 1
                ins.then_inc(routed, 1)
                dve.wait_ge(routed, done)

            dve.wait_ge(S["b_top"], B)
            dve.tensor_tensor(GD[:], TOPV[:, :, 1], TOPV[:, :, 0], ALU.subtract).then_inc(gates_diff, 1)
            for c in range(K):
                one = dve.tensor_tensor(OH[:, c], TOPI[:, :, c].unsqueeze(1).to_broadcast([P, E, NT]),
                                        iota_e[:].unsqueeze(2).to_broadcast([P, E, NT]), ALU.is_equal)
                one.then_inc(oh_made, 1)
            dve.wait_ge(oh_made, K)
            dve.tensor_tensor(CNT[:], OH[:, 0], OH[:, 1], ALU.add).then_inc(counts_made, 1)
            dve.wait_ge(counts_ps, 1)
            chain(dve.tensor_copy(TOT[:], bank[1][:, 0:E * NT]))
            chain(dve.tensor_tensor_scan(CUM[:], ONEf[:], TOT[:], 0.0, ALU.mult, ALU.add))
            chain(dve.tensor_tensor(CUM[:], CUM[:], TOT[:], ALU.subtract))
            chain(dve.tensor_tensor(BASE[:], bank[0][:, 0:E * NT], CUM[:], ALU.add))
            for c in range(K):
                ins = dve.tensor_tensor(PRD[:, c].rearrange("p e t -> p (e t)"), BASE[:],
                                        OH[:, c].rearrange("p e t -> p (e t)"), ALU.mult)
            chain(ins)
            for c in range(K):
                ins = dve.tensor_reduce(POSf[:, c, :], PRD[:, c].rearrange("p e t -> p t e"), AX.X, ALU.add)
            chain(ins)
            chain(dve.tensor_copy(POSu[:], POSf[:].rearrange("p c t -> p (c t)")))
            dve.tensor_scalar(LOu[:], POSu[:], P - 1, None, ALU.bitwise_and)
            chain(dve.tensor_scalar(HIu[:], POSu[:], P.bit_length() - 1, None, ALU.logical_shift_right))
            dve.tensor_copy(LOf[:], LOu[:])
            chain(dve.tensor_copy(HIf[:], HIu[:]))
            dve.scalar_tensor_tensor(EIDX[:], LOf[:], float(NS), HIf[:], ALU.mult, ALU.add)
            for j in range(K * NT):
                dve.tensor_scalar(OHLO[:, j, :], iota_lo[:], LOf[:, j:j + 1], None, ALU.is_equal)
                dve.tensor_scalar(OHHI[:, j, 0:NS], iota_lo[:, 0:NS], HIf[:, j:j + 1], float(j % NT),
                                  ALU.is_equal, ALU.mult)
                dve.tensor_scalar(OHHI[:, j, NS:], iota_lo[:, 0:NS], HIf[:, j:j + 1], iota_part[:, 0:1],
                                  ALU.is_equal, ALU.mult).then_inc(onehots, 1)
            dve.wait_ge(gates_exp, 1)
            chain(dve.tensor_scalar(GS[:], GE[:], 1.0, None, ALU.add))
            chain(dve.reciprocal(GW[:, 0, :], GS[:]))
            chain(dve.tensor_tensor(GW[:, 1, :], GE[:], GW[:, 0, :], ALU.mult))
            dve.wait_ge(ids_ps, 1)
            chain(dve.tensor_copy(SIDXf[:], bank[2][:, 0:NS]))
            dve.scalar_tensor_tensor(SIDX[:], bank[2][:, NS:2 * NS], float(NT), SIDXf[:], ALU.mult, ALU.add)\
                .then_inc(ids_ready, 1)

            def slot_b(s):
                if st := item(s, 2):
                    dve.wait_ge(F["f_out_ps"], st.t + 1)
                    if has_prior(st, 2):
                        dve.wait_ge(eo_stored[st.k % 2], 16 * st.pair)
                    dve.tensor_copy(eo[st.k % 2][:], bank[6 + st.k % 2].rearrange("p (n d) -> p n d", n=G))\
                        .then_inc(F["f_eo"], 1)
                if st := item(s, 0):
                    i = st.k % 2
                    dve.wait_ge(F["f_xgT_ps"], st.t + 1)
                    dve.tensor_copy(xgT[i][:], bank[i]).then_inc(F["f_xgT"], 1)

            run_slots(dve, NG, 2, 4, slot_b)

            def slot_c(s):
                if st := item(s, 3):
                    i = st.k % 2
                    dve.wait_ge(C["c_qke"], st.t + 1)
                    eq_ = [qke[i][:, n, 0:D].rearrange("p (h d) -> p h d", d=HD) for n in range(TPB)]
                    ek_ = [qke[i][:, n, D:].rearrange("p (h d) -> p h d", d=HD) for n in range(TPB)]
                    for n in range(TPB):
                        if has_prior(st, 1):
                            dve.wait_ge(C["c_tv_ps"], TPB * st.t - TPB + n + 1)
                        dve.tensor_tensor(
                            p1[n][:].rearrange("p (h d e) -> p h d e", h=HEADS, d=HD),
                            ek_[n].unsqueeze(3).to_broadcast([P, HEADS, HD, HD]),
                            vc[i][:, n, :].rearrange("p (h e) -> p h e", e=HD).unsqueeze(2)
                            .to_broadcast([P, HEADS, HD, HD]), ALU.mult).then_inc(C["c_p1"], 1)
                    for n in range(TPB):
                        dve.tensor_reduce(ksum[i][:, n, :], ek_[n].rearrange("p h d -> p d h"), AX.X, ALU.add)\
                            .then_inc(C["c_ksum"], 1)
                        dve.tensor_reduce(qsum[i][:, n, :], eq_[n], AX.X, ALU.add).then_inc(C["c_qsum"], 1)
                    dve.wait_ge(C["c_ksum"], TPB * st.t + TPB)
                    dve.reciprocal(rks[i][:], ksum[i][:]).then_inc(C["c_rks"], 1)
                    dve.wait_ge(C["c_qsum"], TPB * st.t + TPB)
                    dve.reciprocal(rqs[i][:], qsum[i][:]).then_inc(C["c_rqs"], 1)
                    dve.wait_ge(C["c_rks"], st.t + 1)
                    dve.wait_ge(C["c_tv_ps"], TPB * st.t + TPB)
                    for n in range(TPB):
                        dve.tensor_tensor(
                            tv[i][:, n, :].rearrange("p (d e) -> p d e", d=HD),
                            bank[3][:, n * HD * HD:(n + 1) * HD * HD].rearrange("p (d e) -> p d e", d=HD),
                            rks[i][:, n, :].unsqueeze(2).to_broadcast([P, HD, HD]), ALU.mult)\
                            .then_inc(C["c_tv"], 1)
                    for n in range(TPB):
                        dve.wait_ge(C["c_tv"], TPB * st.t + n + 1)
                        if has_prior(st, 1):
                            dve.wait_ge(C["c_out_ps"], TPB * st.t - TPB + n + 1)
                        dve.tensor_tensor(
                            p2[n][:].rearrange("p (d h e) -> p d h e", h=HEADS, d=HD),
                            eq_[n].rearrange("p h d -> p d h").unsqueeze(3).to_broadcast([P, HD, HEADS, HD]),
                            tv[i][:, n, :].rearrange("p (d e) -> p d e", d=HD).unsqueeze(2)
                            .to_broadcast([P, HD, HEADS, HD]), ALU.mult).then_inc(C["c_p2"], 1)
                if st := item(s, 4):
                    i = st.k % 2
                    dve.wait_ge(C["c_out_ps"], TPB * st.t + TPB)
                    dve.wait_ge(C["c_rqs"], st.t + 1)
                    dve.tensor_tensor(
                        ao[i][:].rearrange("p n (h e) -> p n h e", e=HD),
                        bank[4][:, 0:TPB * D].rearrange("p (n h e) -> p n h e", n=TPB, e=HD),
                        rqs[i][:].unsqueeze(3).to_broadcast([P, TPB, HEADS, HD]), ALU.mult)\
                        .then_inc(C["c_ao"], 1)
                    dve.wait_ge(C["c_ao"], st.t + 1)
                    dve.tensor_tensor(x3[st.k][:], ao[i][:], x2[st.k][:], ALU.add).then_inc(C["c_x3"], 1)
                    wait_alone(dve, C["c_x3"], st.t + 1)
                    norm_stats(st, C, ("d_stats", "d_mv"), lambda n: x3[st.k][:, n, :], stats2, mv2)
                if st := item(s, 0):
                    i, i4 = st.k % 2, st.k
                    dve.wait_ge(ge_in[i], 16 * TPB * K * (st.pair + 1))
                    for n in range(TPB):
                        dve.scalar_tensor_tensor(xs[i][:, n, :], ge[i][:, n, :],
                                                 GW[:, 0, bass.ds(st.t * TPB + n, 1)],
                                                 X[:, st.t * TPB + n, :], ALU.mult, ALU.add).then_inc(C["c_half"], 1)
                    dve.wait_ge(C["c_half"], TPB * st.t + TPB)
                    for n in range(TPB):
                        dve.scalar_tensor_tensor(x2[i4][:, n, :], ge[i][:, TPB + n, :],
                                                 GW[:, 1, bass.ds(st.t * TPB + n, 1)],
                                                 xs[i][:, n, :], ALU.mult, ALU.add)\
                            .then_inc(C["c_x2" + "_1" * (n == 0)], 1)
                    wait_alone(dve, C["c_x2"], st.t + 1)
                    norm_stats(st, C, ("c_stats", "c_mv"), lambda n: x2[i4][:, n, :], stats, mv)
                if st := item(s, 1):
                    if has_prior(st, 2):
                        dve.wait_ge(C["c_y3T_ps"], st.t - 1)
                    norm_apply(st, C, "c_rstd", "c_y3", lambda n: x2[st.k][:, n, :], mv, rstd, y3)
                if st := item(s, 2):
                    i = st.k % 2
                    dve.wait_ge(C["c_proj"], st.t + 1)
                    q_ = psum[:, 1:3, 0:D].rearrange("p n (h d) -> p n h d", d=HD)
                    k_ = psum[:, 1:3, D:2 * D].rearrange("p n (h d) -> p n h d", d=HD)
                    dve.tensor_reduce(qmax[i][:], q_, AX.X, ALU.max).then_inc(C["c_qmax"], 1)
                    dve.tensor_reduce(kmax[i][:], k_.rearrange("p n h d -> p n d h"), AX.X, ALU.max)\
                        .then_inc(C["c_kmax"], 1)
                    dve.wait_ge(C["c_qmax"], st.t + 1)
                    if has_prior(st, 2):
                        dve.wait_ge(C["c_qke"], st.t - 1)
                    dve.tensor_tensor(qk[i][:, :, 0:D].rearrange("p n (h d) -> p n h d", d=HD), q_,
                                      qmax[i][:].unsqueeze(3).to_broadcast([P, TPB, HEADS, HD]),
                                      ALU.subtract).then_inc(C["c_qk0"], 1)
                    dve.wait_ge(C["c_kmax"], st.t + 1)
                    for n in range(TPB):
                        ins = dve.tensor_tensor(
                            qk[i][:, n, D:].rearrange("p (h d) -> p h d", d=HD), k_[:, n],
                            kmax[i][:, n, :].unsqueeze(1).to_broadcast([P, HEADS, HD]), ALU.subtract)
                    ins.then_inc(C["c_qk"], 1)
                if st := item(s, 5):
                    i = st.k % 2
                    now, prev = y4T[i][:, 1:], y4T[i][:, 0:T]
                    dve.wait_ge(C["d_y4T"], st.t + 1)
                    dve.tensor_tensor(dx[i][:], now, prev, ALU.subtract).then_inc(C["d_dx"], 1)
                    dve.wait_ge(C["d_dx"], st.t + 1)
                    if has_prior(st, 2):
                        dve.wait_ge(C["d_rk_ps"], st.t - 1)
                    dve.scalar_tensor_tensor(xr[i][:], dx[i][:], MU[:, 0:1], prev, ALU.mult, ALU.add)\
                        .then_inc(C["d_mix0"], 1)
                    dve.scalar_tensor_tensor(xk[i][:], dx[i][:], MU[:, 1:2], prev, ALU.mult, ALU.add)\
                        .then_inc(C["d_mix"], 1)
                if st := item(s, 4):
                    if has_prior(st, 2):
                        dve.wait_ge(C["d_y4T_ps"], st.t - 1)
                    norm_apply(st, C, "d_rstd", "d_y4", lambda n: x3[st.k][:, n, :], mv2, rstd2, y4)
                if st := item(s, 6):
                    i = st.k % 2
                    dve.wait_ge(C["d_v_ps"], st.t + 1)
                    dve.scalar_tensor_tensor(rkv[i][:], th[i][:], 1.0,
                                             bank[7][:, 0:TPB * D].rearrange("p (n d) -> p n d", n=TPB),
                                             ALU.add, ALU.mult).then_inc(C["d_rkv"], 1)
                    dve.wait_ge(C["d_rkv"], st.t + 1)
                    if has_prior(st, 2):
                        dve.wait_ge(out_stored[i], 16 * st.pair)
                    dve.tensor_tensor(fin[i][:], rkv[i][:], x3[st.k][:], ALU.add).then_inc(C["d_fin"], 1)

            dve.tensor_scalar(W[:, cFV:cFV + D], W[:, cFV:cFV + D], 0.5, None, ALU.mult).then_inc(C["c_heads"], 1)
            run_slots(dve, B, 6, 4, slot_c)

        @block.tensor
        def _(pe):
            def transposes(st, sems, ready, done, dst, src):
                pe.wait_ge(sems[ready], st.t + 1)
                for n in range(TPB):
                    ins = pe.transpose(dst[:, n * P:(n + 1) * P], src(n), ident[:])
                ins.then_inc(sems[done], 1)

            pe.wait_ge(weights_in, 32)
            pe.wait_ge(consts_made, consts)

            def slot_a(s):
                if st := item(s, 1):
                    if has_prior(st, 1):
                        pe.wait_ge(S["a_xnT"], st.t)
                    transposes(st, S, "a_xn", "a_xnT_ps", bank[0], lambda n: xn[st.k % 2][:, n, :])
                if st := item(s, 2):
                    i = st.k % 2
                    pe.wait_ge(S["a_elu"], st.t + 1)
                    if has_prior(st, 1):
                        pe.wait_ge(S["a_kv"], st.t)
                    for n in range(TPB):
                        ins = pe.matmul(bank[3][:, 0:D + 1], kt[i][:, n, :], vt[i][:, n, :],
                                        start=(n == 0), stop=(n == TPB - 1))
                    ins.then_inc(S["a_kv_ps"], 1)
                if st := item(s, 4):
                    if has_prior(st, 1):
                        pe.wait_ge(S["b_lg"], st.t)
                    transposes(st, S, "b_xm", "b_xmT_ps", bank[7], lambda n: xm[st.k % 2][:, n, :])
                if st := item(s, 1):
                    i = st.k % 2
                    pe.wait_ge(S["a_xnT"], st.t + 1)
                    if has_prior(st, 1):
                        pe.wait_ge(S["a_elu"], st.t)
                    pe.matmul(bank[1][:, 0:T], W[:, cQ:cQ + D], xnT[i][:], start=True, stop=True)
                    for n in range(TPB):
                        ins = pe.matmul(bank[2][:, 2 * D * n:2 * D * (n + 1)], xnT[i][:, n * P:(n + 1) * P],
                                        W[:, cKV:cKV + 2 * D], start=True, stop=True)
                    ins.then_inc(S["a_proj"], 1)
                if st := item(s, 3):
                    i = st.k % 2
                    pe.wait_ge(S["a_attT"], st.t + 1)
                    if has_prior(st, 1):
                        pe.wait_ge(S["a_x1"], st.t)
                    for n in range(TPB):
                        ins = pe.matmul(bank[6][:, n * D:(n + 1) * D], attT[i][:, n * P:(n + 1) * P],
                                        W[:, cO:cO + D], start=True, stop=True)
                    ins.then_inc(S["a_wo"], 1)
                if st := item(s, 2):
                    i = st.k % 2
                    pe.wait_ge(S["a_kv"], st.t + 1)
                    if has_prior(st, 1):
                        pe.wait_ge(S["a_att"], st.t)
                    w = D + HEADS
                    for n in range(TPB):
                        ins = pe.matmul(bank[4][:, n * w:(n + 1) * w], qT[i][:, n * P:(n + 1) * P], kv[i][:],
                                        start=True, stop=True)
                    ins.then_inc(S["a_num"], 1)
                if st := item(s, 4):
                    i = st.k % 2
                    pe.wait_ge(S["b_xmT"], st.t + 1)
                    for n in range(TPB):
                        ins = pe.matmul(bank[7][:, n * E:(n + 1) * E], xmT[i][:, n * P:(n + 1) * P],
                                        W[:, cR:cR + E], start=True, stop=True)
                    ins.then_inc(S["b_logits"], 1)
                if st := item(s, 2):
                    if has_prior(st, 1):
                        pe.wait_ge(S["a_attT"], st.t)
                    transposes(st, S, "a_att", "a_attT_ps", bank[5], lambda n: att[st.k % 2][:, n, :])

            run_slots(pe, B, 4, 2, slot_a)

            pe.wait_ge(counts_made, 1)
            cnt = CNT[:].rearrange("p e t -> p (e t)")
            pe.matmul(bank[0][:, 0:E * NT], before[:], cnt, start=True, stop=True)
            pe.matmul(bank[1][:, 0:E * NT], ones[:], cnt, start=True, stop=True).then_inc(counts_ps, 1)
            for j in range(K * NT):
                pe.wait_ge(onehots, j + 1)
                ins = pe.matmul(bank[2][:, 0:2 * NS], OHLO[:, j, :], OHHI[:, j, :],
                                start=(j == 0), stop=(j == K * NT - 1))
            ins.then_inc(ids_ps, 1)

            def slot_b(s):
                if st := item(s, 0):
                    i = st.k % 2
                    pe.wait_ge(xg_in[i], 16 * G * (st.pair + 1))
                    if has_prior(st, 2):
                        pe.wait_ge(F["f_xgT"], st.t - 1)
                    for n in range(G):
                        ins = pe.transpose(bank[i][:, n * P:(n + 1) * P], xg[i][:, n, :], ident[:])
                    ins.then_inc(F["f_xgT_ps"], 1)
                if st := item(s, 1):
                    i, half = st.k % 2, (st.k // 2) % 2
                    pe.wait_ge(F["f_xgT"], st.t + 1)
                    if st.k % 2 == 0:
                        pe.wait_ge(w_in[half], 32 * (st.quad + 1))
                    for f in range(FB):
                        if has_prior(st, 1):
                            pe.wait_ge(F["f_h"], FB * st.t - FB + f + 1)
                        pe.matmul(bank[2 + f], W1s[half][:, f * P:(f + 1) * P], xgT[i][:],
                                  start=True, stop=True).then_inc(F["f_h_ps"], 1)
                if st := item(s, 2):
                    i, half = st.k % 2, (st.k // 2) % 2
                    pe.wait_ge(F["f_h"], FB * st.t + FB)
                    if has_prior(st, 2):
                        pe.wait_ge(F["f_eo"], st.t - 1)
                    for n in range(G):
                        for f in range(FB):
                            ins = pe.matmul(bank[6 + i][:, n * D:(n + 1) * D], h[i][:, f, n * P:(n + 1) * P],
                                            W2s[half][:, f, :], start=(f == 0), stop=(f == FB - 1))
                    ins.then_inc(F["f_out_ps"], 1)

            run_slots(pe, NG, 2, 4, slot_b)

            pe.wait_ge(C["c_heads"], 1)
            pe.wait_ge(F["f_eo"], NG)

            def slot_c(s):
                if st := item(s, 2):
                    if has_prior(st, 1):
                        pe.wait_ge(C["c_y3T"], st.t)
                    if has_prior(st, 4):
                        pe.wait_ge(C["d_y4T"], st.t - 3)
                    transposes(st, C, "c_y3", "c_y3T_ps", bank[0], lambda n: y3[st.k % 2][:, n, :])
                if st := item(s, 6):
                    i = st.k % 2
                    pe.wait_ge(C["d_mix"], st.t + 1)
                    if has_prior(st, 1):
                        pe.wait_ge(C["d_rkv"], st.t)
                    pe.matmul(bank[5][:, 0:T], W[:, cFK:cFK + D], xk[i][:], start=True, stop=True)
                    for n in range(TPB):
                        ins = pe.matmul(bank[6][:, n * D:(n + 1) * D], xr[i][:, n * P:(n + 1) * P],
                                        W[:, cFR:cFR + D], start=True, stop=True)
                    ins.then_inc(C["d_rk_ps"], 1)
                if st := item(s, 2):
                    i = st.k % 2
                    pe.wait_ge(C["c_y3T"], st.t + 1)
                    if has_prior(st, 1):
                        pe.wait_ge(C["c_v"], st.t)
                    for n in range(TPB):
                        ins = pe.matmul(bank[1 + n][:, 0:3 * D], y3T[i][:, n * P:(n + 1) * P],
                                        W[:, cQKV:cQKV + 3 * D], start=True, stop=True)
                    ins.then_inc(C["c_proj"], 1)
                if st := item(s, 3):
                    for n in range(TPB):
                        pe.wait_ge(C["c_p1"], TPB * st.t + n + 1)
                        if has_prior(st, 1):
                            pe.wait_ge(C["c_tv"], TPB * st.t)
                        w = HD * HD
                        for c in range(HEADS):
                            ins = pe.matmul(bank[3][:, n * w:(n + 1) * w], ident[:], p1[n][:, c * w:(c + 1) * w],
                                            start=(c == 0), stop=(c == HEADS - 1))
                        ins.then_inc(C["c_tv_ps"], 1)
                if st := item(s, 5):
                    if has_prior(st, 1):
                        pe.wait_ge(C["d_y4T"], st.t)
                    pe.wait_ge(C["c_y3T"], st.t + 4 if st.steady else min(st.t + 4, B))
                    transposes(st, C, "d_y4", "d_y4T_ps", bank[0][:, T:], lambda n: y4[st.k % 2][:, n, :])
                if st := item(s, 3):
                    for n in range(TPB):
                        pe.wait_ge(C["c_p2"], TPB * st.t + n + 1)
                        if has_prior(st, 1):
                            pe.wait_ge(C["c_ao"], st.t)
                        for c in range(HD):
                            ins = pe.matmul(bank[4][:, n * D:(n + 1) * D], ident[:], p2[n][:, c * D:(c + 1) * D],
                                            start=(c == 0), stop=(c == HD - 1))
                        ins.then_inc(C["c_out_ps"], 1)
                if st := item(s, 6):
                    i = st.k % 2
                    pe.wait_ge(C["d_ka"], st.t + 1)
                    for n in range(TPB):
                        ins = pe.matmul(bank[7][:, n * D:(n + 1) * D], ka[i][:, n * P:(n + 1) * P],
                                        W[:, cFV:cFV + D], start=True, stop=True)
                    ins.then_inc(C["d_v_ps"], 1)

            run_slots(pe, B, 6, 2, slot_c)


def kernel(**inputs):
    import numpy as np
    import concourse.bacc as bacc
    from concourse.bass_utils import run_bass_kernel_spmd

    x = np.asarray(inputs["L0_attn_x"])
    tiles = x.shape[0] * x.shape[1] // P

    def t(name):
        return np.asarray(inputs[name]).T

    arrays = {
        "x": np.ascontiguousarray(x.reshape(tiles, P, D).transpose(1, 0, 2)),
        "wa": np.ascontiguousarray(np.concatenate(
            [t("L0_attn_w_qkv"), t("L0_attn_w_out"), t("L0_ffn_Wr"), t("L1_attn_W_Q"), t("L1_attn_W_K"),
             t("L1_attn_W_V"), t("L1_ffn_W_r"), t("L1_ffn_W_k"), t("L1_ffn_W_v")], axis=1)),
        "w1": np.ascontiguousarray(inputs["L0_ffn_W1"]),
        "w2": np.ascontiguousarray(np.asarray(inputs["L0_ffn_W2"]).reshape(8, 4, P, D).transpose(0, 2, 1, 3)),
        "mu": np.ascontiguousarray(np.stack([inputs["L1_ffn_mu_r"], inputs["L1_ffn_mu_k"]], axis=1)),
    }
    nc = bacc.Bacc("TRN2", target_bir_lowering=False, num_devices=1)
    args = [nc.dram_tensor(name, a.shape, F32, kind="ExternalInput").ap() for name, a in arrays.items()]
    out = nc.dram_tensor("out", (P, tiles, D), F32, kind="ExternalOutput").ap()
    build(nc, *args, out)
    r = run_bass_kernel_spmd(nc, [arrays], core_ids=[0])
    return r.results[0]["out"].transpose(1, 0, 2).reshape(x.shape)
```

```python
from collections import namedtuple
from contextlib import ExitStack

import concourse.bass as bass
from concourse import mybir

F32 = mybir.dt.float32
BF16 = mybir.dt.bfloat16
F32R = mybir.dt.float32r
U32 = mybir.dt.uint32
ALU = mybir.AluOpType
ACT = mybir.ActivationFunctionType
AX = mybir.AxisListType

P = 128
D = 128
HEADS = 16
HD = D // HEADS
EPS = 1e-5

Slot = namedtuple("Slot", "m k unroll steady count")
Step = namedtuple("Step", "t pair quad k steady")


def run_slots(eng, count, unroll, stages):
    last_lag = max(lag for _, lag in stages)

    def body(slot):
        for stage, lag in stages:
            if st := item(slot, lag):
                stage(st)

    peeled = -(-(last_lag + 2) // unroll)
    for m in range(peeled):
        for k in range(unroll):
            body(Slot(m, k, unroll, False, count))
    with eng.Fori(peeled, count // unroll) as m:
        for k in range(unroll):
            body(Slot(m, k, unroll, True, count))
    for s in range(count, count + last_lag):
        body(Slot(s // unroll, s % unroll, unroll, False, count))


def item(slot, lag):
    j = slot.k - lag
    t = slot.unroll * slot.m + j
    if not slot.steady and not 0 <= t < slot.count:
        return None
    return Step(t, (slot.unroll // 2) * slot.m + j // 2, slot.m + j // 4, j % slot.unroll, slot.steady)


def has_prior(st, n):
    return st.steady or st.t >= n


def build(nc, x, wa, w1, w2, mu, out):
    B, T = 16, 256
    TPB = T // P
    N = B * T
    NT = N // P
    E, FF = w1.shape[0], w1.shape[2]
    FB = FF // P
    K = 2
    NS = N * K // P
    G = 4
    NG = NS // G
    GPC = NG // E
    assert GPC == 2 and TPB == 2

    cQ, cKV, cO, cR = 0, D, 3 * D, 4 * D
    cQKV = cR + E
    cFR = cQKV + 3 * D
    cFK, cFV = cFR + D, cFR + 2 * D
    cEnd = cFR + 3 * D
    CH = 4
    CW = K * NT // CH
    GATE_CHUNKS = ((0, 1), (2,), (3,))
    assert wa.shape == (P, cEnd)

    xn_dram = nc.dram_tensor("xn_dram", (P * NT, D), F32).ap()
    eo_dram = nc.dram_tensor("eo_dram", (P * NS, D), F32).ap()
    xn_rows = xn_dram.rearrange("(p t) d -> p t d", p=P)
    eo_rows = eo_dram.rearrange("(p t) d -> p t d", p=P)

    with ExitStack() as ctx:
        def sb(name, shape, dt=F32):
            return ctx.enter_context(nc.sbuf_tensor(name, shape, dt))

        def two(name, shape, dt=F32):
            return [sb(f"{name}{i}", shape, dt) for i in range(2)]

        def sem(name):
            return ctx.enter_context(nc.semaphore(name))

        psum = ctx.enter_context(nc.psum_tensor("psum", [P, 8, 512], F32))
        bank = [psum[:, i, :] for i in range(8)]

        W = sb("W", [P, cEnd])
        WP = sb("WP", [P, 2 * D])
        MU = sb("MU", [P, 2])
        OMM = sb("OMM", [P, 2])
        ident = sb("ident", [P, P])
        block_mask = sb("block_mask", [P, D + HEADS])
        neg_half = sb("neg_half", [P, TPB])
        iota_e = sb("iota_e", [P, E])
        before = sb("before", [P, P], BF16)
        ones = sb("ones", [P, P], BF16)
        iota_lo = sb("iota_lo", [P, P])
        iota_tile = sb("iota_tile", [P, NT])
        iota_part = sb("iota_part", [P, 1])
        y4T = two("y4T", [P, 1 + T])
        vt = two("vt", [P, TPB, D + 1])
        ONEf = sb("ONEf", [P, E * NT])

        X = sb("X", [P, NT, D])
        LG = sb("LG", [P, E, NT])
        EIDX = sb("EIDX", [P, K * NT], U32)
        SIDX = sb("SIDX", [P, NS], U32)
        WS = sb("WS", [P, NS])
        SIDX_col = two("SIDX_col", [P, G], U32)
        EIDX_col = [sb(f"EIDX_col{i}", [P, TPB * K], U32) for i in range(4)]

        xm = two("xm", [P, TPB, D])

        def norm_buffers(i):
            return dict(stats=two(f"stats{i}", [P, TPB, 6]), mv=two(f"mv{i}", [P, TPB, 2]),
                        veps=two(f"veps{i}", [P, TPB]), nmean=two(f"nmean{i}", [P, TPB]),
                        rstd=two(f"rstd{i}", [P, TPB]), nmr=two(f"nmr{i}", [P, TPB]))

        norm1, norm2 = norm_buffers(1), norm_buffers(2)

        W1s = two("W1s", [P, FF])
        W2s = two("W2s", [P, FB * D])
        W1hi, W1lo = two("W1hi", [P, FF], F32R), two("W1lo", [P, FF], F32R)
        xhi, xlo = two("xhi", [P, G * P], F32R), two("xlo", [P, G * P], F32R)
        h = two("h", [P, FB, G * P])
        xg = two("xg", [P, G, D])
        eo = two("eo", [P, G, D])

        outer, ctx_a = ctx, ExitStack()
        ctx = ctx_a
        xn = two("xn", [P, TPB, D])
        xnT = two("xnT", [P, T])
        eq = two("eq", [P, T + TPB * D])
        em = two("em", [P, T + TPB * D])
        qT = two("qT", [P, T])
        kt = two("kt", [P, TPB, D])
        kv = two("kv", [P, D + HEADS])
        den = two("den", [P, TPB, HEADS])
        rden = two("rden", [P, TPB, HEADS])
        att = two("att", [P, TPB, D])
        attT = two("attT", [P, T])
        xmT = two("xmT", [P, T])
        ctx_a.close()

        ctx = ctx_r = ExitStack()
        lg = sb("lg", [P, E, NT])
        top = [sb(f"top{c}", [P, NT]) for c in range(K)]
        hit = sb("hit", [P, E, NT])
        numb = sb("numb", [P, E, NT])
        which = sb("which", [P, NT])
        OH = sb("OH", [P, K, E, NT])
        CNT = sb("CNT", [P, E, NT], BF16)
        TOT = sb("TOT", [P, E * NT])
        CUM = sb("CUM", [P, E * NT])
        BASE = sb("BASE", [P, E * NT])
        PRD = sb("PRD", [P, K, E, NT])
        POSf = sb("POSf", [P, K, NT])
        POSu = sb("POSu", [P, K * NT], U32)
        LOu = sb("LOu", [P, K * NT], U32)
        HIu = sb("HIu", [P, K * NT], U32)
        LOf = sb("LOf", [P, K * NT])
        HIf = sb("HIf", [P, K * NT])
        GD = sb("GD", [P, NT])
        GE = sb("GE", [P, NT])
        GS = sb("GS", [P, NT])
        GW = sb("GW", [P, K, NT])
        OHLO = sb("OHLO", [P, K * NT, P], BF16)
        OHHI = sb("OHHI", [P, K * NT, NS], BF16)
        OHID = sb("OHID", [P, K * NT, 2 * NS], BF16)
        OHW = sb("OHW", [P, K * NT, 3 * NS], BF16)
        gate_part = [sb(f"gate_part{i}", [P, K * NT], BF16) for i in range(3)]
        gate_rest = sb("gate_rest", [P, K * NT])
        gate_sum = sb("gate_sum", [P, NS])
        SIDXf = sb("SIDXf", [P, NS])
        ctx_r.close()

        ctx = ctx_c = ExitStack()
        x2 = [sb(f"x2_{i}", [P, TPB, D]) for i in range(4)]
        y3 = two("y3", [P, TPB, D])
        y3T = two("y3T", [P, T])
        qmax = two("qmax", [P, TPB, HEADS])
        kmax = two("kmax", [P, TPB, HD])
        qk = two("qk", [P, TPB, 2 * D])
        qke = two("qke", [P, TPB, 2 * D])
        vc = two("vc", [P, TPB, D])
        qsum = two("qsum", [P, TPB, HEADS])
        ksum = two("ksum", [P, TPB, HD])
        rqs = two("rqs", [P, TPB, HEADS])
        rks = two("rks", [P, TPB, HD])
        qn = two("qn", [P, TPB, D])
        p1 = two("p1", [P, TPB, HEADS * HD * HD])
        tv = two("tv", [P, TPB, HD * HD])
        p2 = two("p2", [P, HD * HEADS * HD])
        x3 = two("x3", [P, TPB, D])
        y4 = two("y4", [P, TPB, D])
        kr = two("kr", [P, T])
        ka = two("ka", [P, T])
        th = two("th", [P, TPB, D])
        rkv = two("rkv", [P, TPB, D])
        fin = two("fin", [P, TPB, D])
        ctx_c.close()
        ctx = outer

        weights_in = sem("weights_in")
        consts_made = sem("consts_made")
        x_in = [sem(f"x_in{i}") for i in range(2)]
        norm_names = "stats aggr mv veps nmean rstd nmr"
        S = {n: sem("a_" + n) for n in """xn0 xn xnT_ps xnT proj eq0 eq v em elu0 elu kv_ps kv0 kv num den rden att
            attT_ps attT wo x1 xm0 xm xmT_ps xmT logits lg""".split()}
        N1 = {n: sem("a1_" + n) for n in norm_names.split()}
        N2 = {n: sem("a2_" + n) for n in norm_names.split()}
        N3 = {n: sem("c1_" + n) for n in norm_names.split()}
        N4 = {n: sem("c2_" + n) for n in norm_names.split()}
        xn_stored = [sem(f"xn_stored{i}") for i in range(2)]
        routed = sem("routed")
        counts_made = sem("counts_made")
        counts_ps = sem("counts_ps")
        gates_diff = sem("gates_diff")
        gates_exp = sem("gates_exp")
        hi_made = sem("hi_made")
        lo_made = sem("lo_made")
        by_tile = sem("by_tile")
        by_part = sem("by_part")
        eidx_made = sem("eidx_made")
        ids_ps = sem("ids_ps")
        ids_ready = sem("ids_ready")
        weighted = sem("weighted")
        gates_ps = sem("gates_ps")
        gates_ready = sem("gates_ready")
        w_in = [sem(f"w_in{i}") for i in range(2)]
        F = {n: sem("f_" + n) for n in """idx xgT_ps xhi xlo whi wlo h_ps h out_ps eo""".split()}
        xg_in = [sem(f"xg_in{i}") for i in range(2)]
        eo_stored = [sem(f"eo_stored{i}") for i in range(2)]
        x1_in = [sem(f"x1_in{i}") for i in range(4)]
        e0_in = [sem(f"e0_in{i}") for i in range(2)]
        e1_in = [sem(f"e1_in{i}") for i in range(2)]
        C = {n: sem("c_" + n) for n in """heads idx y30 y3 y3T_ps y3T proj qmax kmax qk0 qk v qke p1 p1_pool ksum qsum
            rks rqs qn tv_ps tv p2_0 p2 out0_ps out_ps x3 y40 y4 y4T_ps y4T rk_ps relu th ka v_ps rkv fin""".split()}
        out_stored = [sem(f"out_stored{i}") for i in range(2)]

        consts = 20

        def wait_alone(eng, sem_, value):
            value = value if isinstance(value, int) else eng.to_reg(value)
            eng.wait_ge(consts_made, consts)
            eng.wait_ge(sem_, value)

        def outer_kv(i, n):
            return (p1[i][:, n, :].rearrange("p (h d e) -> p h d e", h=HEADS, d=HD),
                    qke[i][:, n, D:].rearrange("p (h d) -> p h d", d=HD).unsqueeze(3)
                    .to_broadcast([P, HEADS, HD, HD]),
                    vc[i][:, n, :].rearrange("p (h e) -> p h e", e=HD).unsqueeze(2)
                    .to_broadcast([P, HEADS, HD, HD]))

        block = ctx.enter_context(nc.Block())

        @block.sync
        def _(sp):
            sp.dma_start(W[:], wa).then_inc(weights_in, 16)
            sp.dma_start(MU[:], mu).then_inc(weights_in, 16)

            def load_x(st):
                if has_prior(st, 2):
                    wait_alone(sp, x_in[st.k % 2], 16 * st.pair)
                sp.dma_start(X[:, bass.ts(st.t, TPB), :], x[:, bass.ts(st.t, TPB), :])\
                    .then_inc(x_in[st.k % 2], 16)

            def store_xn(st):
                if has_prior(st, 2):
                    wait_alone(sp, xn_stored[st.k % 2], 16 * st.pair)
                wait_alone(sp, S["xm"], st.t + 1)
                sp.dma_start(xn_rows[:, bass.ts(st.t, TPB), :], xm[st.k % 2][:])\
                    .then_inc(xn_stored[st.k % 2], 16)

            run_slots(sp, B, 2, [(load_x, 0), (store_xn, 8)])

            def load_weights(st):
                if st.k % 2 == 0:
                    half = (st.k // 2) % 2
                    if has_prior(st, 4):
                        wait_alone(sp, F["out_ps"], st.t - 2)
                    sp.dma_start(W1s[half][:], w1[st.pair]).then_inc(w_in[half], 16)
                    sp.dma_start(W2s[half][:].rearrange("p (f d) -> p f d", f=FB), w2[st.pair])\
                        .then_inc(w_in[half], 16)

            def store_experts(st):
                if has_prior(st, 2):
                    wait_alone(sp, eo_stored[st.k % 2], 16 * st.pair)
                wait_alone(sp, F["eo"], st.t + 1)
                sp.dma_start(eo_rows[:, bass.ts(st.t, G), :], eo[st.k % 2][:])\
                    .then_inc(eo_stored[st.k % 2], 16)

            run_slots(sp, NG, 4, [(load_weights, 0), (store_experts, 4)])

            def load_x1(st):
                if has_prior(st, 4):
                    wait_alone(sp, C["out_ps"], st.t - 3)
                    sp.wait_ge(C["out0_ps"], st.t - 3)
                sp.dma_start(x2[st.k][:], X[:, bass.ts(st.t, TPB), :]).then_inc(x1_in[st.k], 16)

            def store_out(st):
                if has_prior(st, 2):
                    wait_alone(sp, out_stored[st.k % 2], 16 * st.pair)
                wait_alone(sp, C["fin"], st.t + 1)
                sp.dma_start(out[:, bass.ts(st.t, TPB), :], fin[st.k % 2][:])\
                    .then_inc(out_stored[st.k % 2], 16)

            run_slots(sp, B, 4, [(load_x1, 0), (store_out, 6)])
            for s in out_stored:
                sp.wait_ge(s, 16 * B // 2)

        @block.gpsimd
        def _(pool):
            pool.memset(ident[:], 0.0).then_inc(consts_made, 1)
            pool.memset(block_mask[:], 1.0).then_inc(consts_made, 1)
            pool.memset(before[:], 1.0).then_inc(consts_made, 1)
            pool.memset(ones[:], 1.0).then_inc(consts_made, 1)
            pool.memset(ONEf[:], 1.0).then_inc(consts_made, 1)
            pool.memset(neg_half[:], -0.5).then_inc(consts_made, 1)
            for v in vt:
                pool.memset(v[:, :, D:D + 1], 1.0).then_inc(consts_made, 1)
            for y in y4T:
                pool.memset(y[:, 0:1], 0.0).then_inc(consts_made, 1)
            pool.iota(iota_e[:], [[-1, E]], base=E, channel_multiplier=0,
                      allow_small_or_imprecise_dtypes=True).then_inc(consts_made, 1)
            pool.iota(iota_lo[:], [[1, P]], base=0, channel_multiplier=0,
                      allow_small_or_imprecise_dtypes=True).then_inc(consts_made, 1)
            pool.iota(iota_tile[:], [[1, NT]], base=0, channel_multiplier=0,
                      allow_small_or_imprecise_dtypes=True).then_inc(consts_made, 1)
            pool.iota(iota_part[:], [[0, 1]], base=0, channel_multiplier=1,
                      allow_small_or_imprecise_dtypes=True).then_inc(consts_made, 1)
            pool.wait_ge(consts_made, 14)
            pool.affine_select(out=ident[:], in_=ident[:], compare_op=ALU.not_equal, fill=1.0, base=0,
                               pattern=[[-1, P]], channel_multiplier=1).then_inc(consts_made, 1)
            pool.affine_select(out=before[:], in_=before[:], compare_op=ALU.is_gt, fill=0.0, base=0,
                               pattern=[[1, P]], channel_multiplier=-1).then_inc(consts_made, 1)
            by_head = block_mask[:, 0:D].rearrange("p (h j) -> p h j", j=HD)
            heads = block_mask[:, D:D + HEADS]
            pool.affine_select(out=by_head, in_=by_head, compare_op=ALU.is_ge, fill=0.0, base=0,
                               pattern=[[-HD, HEADS], [0, HD]], channel_multiplier=1).then_inc(consts_made, 1)
            pool.affine_select(out=heads, in_=heads, compare_op=ALU.is_ge, fill=0.0, base=0,
                               pattern=[[-HD, HEADS]], channel_multiplier=1).then_inc(consts_made, 1)
            pool.wait_ge(consts_made, 18)
            pool.affine_select(out=by_head, in_=by_head, compare_op=ALU.is_ge, fill=0.0, base=HD - 1,
                               pattern=[[HD, HEADS], [0, HD]], channel_multiplier=-1).then_inc(consts_made, 1)
            pool.affine_select(out=heads, in_=heads, compare_op=ALU.is_ge, fill=0.0, base=HD - 1,
                               pattern=[[HD, HEADS]], channel_multiplier=-1).then_inc(consts_made, 1)
            pool.wait_ge(consts_made, consts)

            def rsqrt(st, nb, norm, used, used_):
                i = st.k % 2
                wait_alone(pool, norm["mv"], st.t + 1)
                pool.tensor_scalar(nb["veps"][i][:], nb["mv"][i][:, :, 1], EPS, 1.0, ALU.add, ALU.mult)\
                    .then_inc(norm["veps"], 1)
                pool.tensor_scalar(nb["nmean"][i][:], nb["mv"][i][:, :, 0], -1.0, 1.0, ALU.mult, ALU.mult)\
                    .then_inc(norm["nmean"], 1)
                wait_alone(pool, norm["veps"], st.t + 1)
                if has_prior(st, 2):
                    pool.wait_ge(used[used_], st.t - 1)
                pool.tensor_tensor(nb["rstd"][i][:], nb["veps"][i][:], neg_half[:], ALU.pow)\
                    .then_inc(norm["rstd"], 1)
                wait_alone(pool, norm["rstd"], st.t + 1)
                pool.wait_ge(norm["nmean"], st.t + 1)
                pool.tensor_tensor(nb["nmr"][i][:], nb["nmean"][i][:], nb["rstd"][i][:], ALU.mult)\
                    .then_inc(norm["nmr"], 1)

            def rsqrt1(st):
                rsqrt(st, norm1, N1, S, "xn")

            def rsqrt2(st):
                rsqrt(st, norm2, N2, S, "xm")

            run_slots(pool, B, 2, [
                (rsqrt1, 0), (rsqrt2, 4)])

            for q in range(CH):
                cols, tiles = slice(q * CW, (q + 1) * CW), slice(q % (CH // K) * CW, (q % (CH // K) + 1) * CW)
                pool.wait_ge(hi_made, q + 1)
                pool.tensor_tensor(OHID[:, cols, 0:NS], OHHI[:, cols, :],
                                   iota_tile[:, tiles].unsqueeze(2).to_broadcast([P, CW, NS]), ALU.mult)\
                    .then_inc(by_tile, 1)

            pool.wait_ge(ids_ready, 1)
            for s in xn_stored:
                pool.wait_ge(s, 16 * B // 2)

            def gather_rows(st):
                i = st.k % 2
                if has_prior(st, 2):
                    wait_alone(pool, F["xgT_ps"], st.t - 1)
                    pool.wait_ge(xg_in[i], 16 * G * st.pair)
                pool.tensor_copy(SIDX_col[i][:], SIDX[:, bass.ts(st.t, G)]).then_inc(F["idx"], 1)
                wait_alone(pool, F["idx"], st.t + 1)
                for j in range(G):
                    pool.indirect_dma_start(
                        xg[i][:, j, :], None, xn_dram,
                        bass.IndirectOffsetOnAxis(ap=SIDX_col[i][:, j:j + 1], axis=0)).then_inc(xg_in[i], 16)

            run_slots(pool, NG, 4, [(gather_rows, 0)])
            for s in eo_stored:
                pool.wait_ge(s, 16 * NG // 2)

            def gather_first(st):
                i, i4 = st.k % 2, st.k
                for c in range(K):
                    ins = pool.tensor_copy(EIDX_col[i4][:, c * TPB:(c + 1) * TPB],
                                           EIDX[:, bass.ds(st.t * TPB + c * NT, TPB)])
                    ins.then_inc(C["idx"], 1)
                wait_alone(pool, C["idx"], K * st.t + K)
                wait_alone(pool, x1_in[i4], 16 * (st.quad + 1))
                for n in range(TPB):
                    pool.indirect_dma_start(
                        x2[i4][:, n, :], None, eo_dram,
                        bass.IndirectOffsetOnAxis(ap=EIDX_col[i4][:, n:n + 1], axis=0),
                        compute_op=ALU.add).then_inc(e0_in[i], 16)

            def gather_second(st):
                i, i4 = st.k % 2, st.k
                wait_alone(pool, e0_in[i], 16 * TPB * (st.pair + 1))
                for n in range(TPB):
                    pool.indirect_dma_start(
                        x2[i4][:, n, :], None, eo_dram,
                        bass.IndirectOffsetOnAxis(ap=EIDX_col[i4][:, TPB + n:TPB + n + 1], axis=0),
                        compute_op=ALU.add).then_inc(e1_in[i], 16)

            def products_kv(st):
                wait_alone(pool, C["qke"], st.t + 1)
                if has_prior(st, 2):
                    pool.wait_ge(C["tv_ps"], st.t - 1)
                pool.tensor_tensor(*outer_kv(st.k % 2, 1), ALU.mult).then_inc(C["p1_pool"], 1)

            def rsqrt3(st):
                rsqrt(st, norm1, N3, C, "y3")

            def rsqrt4(st):
                rsqrt(st, norm2, N4, C, "y4")

            run_slots(pool, B, 4, [
                (gather_second, 1), (gather_first, 0), (rsqrt3, 1), (products_kv, 2),
                (rsqrt4, 3)])

        @block.scalar
        def _(act):
            def evacuate(st, sems, ready, done, dst, src):
                act.wait_ge(sems[ready], st.t + 1)
                act.activation(dst, src, ACT.Copy).then_inc(sems[done], 1)

            def normalize(st, norm, nb, sems, done, dst, rows):
                i = st.k % 2
                for n in range(TPB):
                    act.activation(dst[i][:, n, :], rows(n), ACT.Identity, scale=nb["rstd"][i][:, n:n + 1],
                                   bias=nb["nmr"][i][:, n:n + 1])\
                        .then_inc(sems[done + "0" * (n == 0)], 1)

            def tiles(ps):
                return ps[:, 0:TPB * D].rearrange("p (n d) -> p n d", n=TPB)

            def apply1(st):
                wait_alone(act, N1["nmr"], st.t + 1)
                if has_prior(st, 2):
                    act.wait_ge(S["xnT_ps"], st.t - 1)
                normalize(st, N1, norm1, S, "xn", xn, lambda n: X[:, st.t * TPB + n, :])

            def evac_xn(st):
                evacuate(st, S, "xnT_ps", "xnT", xnT[st.k % 2][:], bank[0][:, 0:T])

            def evac_xm(st):
                evacuate(st, S, "xmT_ps", "xmT", xmT[st.k % 2][:], bank[7][:, 0:T])

            def evac_att(st):
                evacuate(st, S, "attT_ps", "attT", attT[st.k % 2][:], bank[5][:, 0:T])

            def exps(st):
                i = st.k % 2
                act.wait_ge(S["proj"], st.t + 1)
                if has_prior(st, 2):
                    act.wait_ge(S["em"], st.t - 1)
                    act.wait_ge(S["kv_ps"], st.t - 1)
                kvp = bank[2].rearrange("p (n w d) -> p n w d", n=TPB, w=2)
                act.activation(eq[i][:, 0:T], bank[1][:, 0:T], ACT.Exp).then_inc(S["eq0"], 1)
                act.activation(eq[i][:, T:].rearrange("p (n d) -> p n d", n=TPB), kvp[:, :, 0, :],
                               ACT.Exp).then_inc(S["eq"], 1)
                act.activation(vt[i][:, :, 0:D], kvp[:, :, 1, :], ACT.Copy).then_inc(S["v"], 1)

            def keep_x1(st):
                wait_alone(act, S["wo"], st.t + 1)
                act.activation(X[:, bass.ts(st.t, TPB), :], tiles(bank[6]), ACT.Copy).then_inc(S["x1"], 1)

            def apply2(st):
                wait_alone(act, S["x1"], st.t + 1)
                act.wait_ge(N2["nmr"], st.t + 1)
                if has_prior(st, 2):
                    act.wait_ge(S["xmT_ps"], st.t - 1)
                    act.wait_ge(xn_stored[st.k % 2], 16 * st.pair)
                normalize(st, N2, norm2, S, "xm", xm, lambda n: X[:, st.t * TPB + n, :])

            def keep_logits(st):
                wait_alone(act, S["logits"], st.t + 1)
                act.activation(LG[:, :, bass.ts(st.t, TPB)],
                               bank[7][:, T:T + TPB * E].rearrange("p (n e) -> p e n", n=TPB), ACT.Copy)\
                    .then_inc(S["lg"], 1)

            run_slots(act, B, 2, [
                (apply1, 0), (exps, 1), (evac_att, 3), (evac_xn, 0),
                (evac_xm, 5), (apply2, 4), (keep_x1, 3), (keep_logits, 5)])

            act.wait_ge(gates_diff, 1)
            act.activation(GE[:], GD[:], ACT.Exp).then_inc(gates_exp, 1)
            for q in range(CH):
                cols = slice(q * CW, (q + 1) * CW)
                act.wait_ge(hi_made, q + 1)
                act.activation(OHID[:, cols, NS:], OHHI[:, cols, :], ACT.Copy, scale=iota_part[:, 0:1])\
                    .then_inc(by_part, 1)

            def split_weights(st):
                if st.k % 2 == 0:
                    half = (st.k // 2) % 2
                    act.wait_ge(w_in[half], 32 * (st.quad + 1))
                    if has_prior(st, 4):
                        act.wait_ge(F["h_ps"], FB * (st.t - 2))
                    act.activation(W1hi[half][:], W1s[half][:], ACT.Copy).then_inc(F["whi"], 1)

            def split_x(st):
                i = st.k % 2
                act.wait_ge(F["xgT_ps"], st.t + 1)
                if has_prior(st, 2):
                    act.wait_ge(F["h_ps"], FB * st.t - FB)
                act.activation(xhi[i][:], bank[i], ACT.Copy).then_inc(F["xhi"], 1)

            def gelu(st):
                for f in range(FB):
                    act.wait_ge(F["h_ps"], FB * st.t + f + 1)
                    if f == 0 and has_prior(st, 2):
                        act.wait_ge(F["out_ps"], st.t - 1)
                    act.activation(h[st.k % 2][:, f, :], bank[2 + f], ACT.Gelu).then_inc(F["h"], 1)

            run_slots(act, NG, 4, [
                (split_weights, 0), (split_x, 0), (gelu, 1)])

            def apply3(st):
                wait_alone(act, N3["nmr"], st.t + 1)
                if has_prior(st, 2):
                    act.wait_ge(C["y3T_ps"], st.t - 1)
                normalize(st, N3, norm1, C, "y3", y3, lambda n: x2[st.k][:, n, :])

            def evac_y3(st):
                evacuate(st, C, "y3T_ps", "y3T", y3T[st.k % 2][:], bank[0][:, 0:T])

            def keep_v(st):
                act.wait_ge(C["proj"], st.t + 1)
                if has_prior(st, 2):
                    act.wait_ge(C["p1"], st.t - 1)
                    act.wait_ge(C["p1_pool"], st.t - 1)
                act.activation(vc[st.k % 2][:], psum[:, 1:3, 2 * D:3 * D], ACT.Copy).then_inc(C["v"], 1)

            def exps_qk(st):
                i = st.k % 2
                if has_prior(st, 2):
                    act.wait_ge(C["p1"], st.t - 1)
                    act.wait_ge(C["qn"], st.t - 1)
                    act.wait_ge(C["p1_pool"], st.t - 1)
                act.wait_ge(C["qk"], st.t + 1)
                act.activation(qke[i][:], qk[i][:], ACT.Exp).then_inc(C["qke"], 1)

            def keep_x3(st):
                act.wait_ge(C["out0_ps"], st.t + 1)
                act.wait_ge(C["out_ps"], st.t + 1)
                if has_prior(st, 2):
                    act.wait_ge(C["fin"], st.t - 1)
                act.activation(x3[st.k % 2][:], tiles(bank[4]), ACT.Copy).then_inc(C["x3"], 1)

            def apply4(st):
                wait_alone(act, C["x3"], st.t + 1)
                act.wait_ge(N4["nmr"], st.t + 1)
                if has_prior(st, 2):
                    act.wait_ge(C["y4T_ps"], st.t - 1)
                normalize(st, N4, norm2, C, "y4", y4, lambda n: x3[st.k % 2][:, n, :])

            def evac_y4(st):
                evacuate(st, C, "y4T_ps", "y4T", y4T[st.k % 2][:, 1:], bank[5][:, 0:T])

            def gate_mix(st):
                i = st.k % 2
                act.wait_ge(C["rk_ps"], st.t + 1)
                act.activation(kr[i][:], bank[6][:, T:], ACT.Relu).then_inc(C["relu"], 1)
                act.activation(th[i][:], tiles(bank[6]), ACT.Tanh, scale=0.5).then_inc(C["th"], 1)
                act.wait_ge(C["relu"], st.t + 1)
                act.activation(ka[i][:], kr[i][:], ACT.Square).then_inc(C["ka"], 1)

            run_slots(act, B, 4, [
                (evac_y3, 1), (apply4, 3), (keep_v, 1), (evac_y4, 3),
                (exps_qk, 1), (apply3, 0), (keep_x3, 2), (gate_mix, 3)])

        @block.vector
        def _(dve):
            def norm_stats(st, norm, nb, rows):
                i = st.k % 2
                for n in range(TPB):
                    dve.bn_stats(nb["stats"][i][:, n, :], rows(n)).then_inc(norm["stats"], 1)
                if has_prior(st, 2):
                    wait_alone(dve, norm["nmr"], st.t - 1)
                wait_alone(dve, norm["stats"], TPB * st.t + TPB)
                for n in range(TPB):
                    dve.bn_aggr(nb["mv"][i][:, n, :], nb["stats"][i][:, n, :])\
                        .then_inc(norm["aggr" if n == 0 else "mv"], 1)

            dve.wait_ge(consts_made, consts)
            dve.wait_ge(weights_in, 32)
            dve.tensor_scalar(OMM[:], MU[:], -1.0, 1.0, ALU.mult, ALU.add).then_inc(C["heads"], 1)
            dve.tensor_scalar(W[:, cFV:cFV + D], W[:, cFV:cFV + D], 0.5, None, ALU.mult).then_inc(C["heads"], 1)
            dve.wait_ge(C["heads"], 2)
            for j in range(2):
                dve.tensor_scalar(WP[:, j * D:(j + 1) * D], W[:, cFR + j * D:cFR + (j + 1) * D],
                                  OMM[:, j:j + 1], None, ALU.mult).then_inc(C["heads"], 1)
            for j in range(2):
                cols = W[:, cFR + j * D:cFR + (j + 1) * D]
                dve.tensor_scalar(cols, cols, MU[:, j:j + 1], None, ALU.mult).then_inc(C["heads"], 1)

            def mask_kv(st):
                i = st.k % 2
                dve.wait_ge(S["kv_ps"], st.t + 1)
                if has_prior(st, 2):
                    dve.wait_ge(S["num"], st.t - 1)
                dve.tensor_tensor(kv[i][:, 0:D], bank[3][:, 0:D], block_mask[:, 0:D], ALU.mult)\
                    .then_inc(S["kv0"], 1)
                dve.tensor_scalar(kv[i][:, D:], block_mask[:, D:], bank[3][:, D:D + 1], None, ALU.mult)\
                    .then_inc(S["kv"], 1)

            def stats_x(st):
                wait_alone(dve, x_in[st.k % 2], 16 * (st.pair + 1))
                norm_stats(st, N1, norm1, lambda n: X[:, st.t * TPB + n, :])

            def stats_x1(st):
                wait_alone(dve, S["x1"], st.t + 1)
                norm_stats(st, N2, norm2, lambda n: X[:, st.t * TPB + n, :])

            def divide(st):
                i = st.k % 2
                nd = bank[4][:, 0:TPB * (D + HEADS)].rearrange("p (n c) -> p n c", n=TPB)
                dve.wait_ge(S["num"], st.t + 1)
                dve.tensor_scalar(den[i][:], nd[:, :, D:], 1e-6, None, ALU.max).then_inc(S["den"], 1)
                dve.wait_ge(S["den"], st.t + 1)
                dve.reciprocal(rden[i][:], den[i][:]).then_inc(S["rden"], 1)
                dve.wait_ge(S["rden"], st.t + 1)
                if has_prior(st, 2):
                    dve.wait_ge(S["attT_ps"], st.t - 1)
                dve.tensor_tensor(
                    att[i][:].rearrange("p n (h j) -> p n h j", j=HD),
                    nd[:, :, 0:D].rearrange("p n (h j) -> p n h j", j=HD),
                    rden[i][:].unsqueeze(3).to_broadcast([P, TPB, HEADS, HD]), ALU.mult).then_inc(S["att"], 1)

            def clamp(st):
                i = st.k % 2
                dve.wait_ge(S["eq"], st.t + 1)
                dve.tensor_scalar(em[i][:], eq[i][:], 1.0, None, ALU.min).then_inc(S["em"], 1)

            def elu(st):
                i = st.k % 2
                dve.wait_ge(S["em"], st.t + 1)
                dve.wait_ge(S["v"], st.t + 1)
                if has_prior(st, 2):
                    dve.wait_ge(S["num"], st.t - 1)
                kvp = bank[2].rearrange("p (n w d) -> p n w d", n=TPB, w=2)
                dve.scalar_tensor_tensor(kt[i][:], kvp[:, :, 0, :], 1.0,
                                         em[i][:, T:].rearrange("p (n d) -> p n d", n=TPB),
                                         ALU.add, ALU.max).then_inc(S["elu0"], 1)
                dve.scalar_tensor_tensor(qT[i][:], bank[1][:, 0:T], 1.0, em[i][:, 0:T], ALU.add, ALU.max)\
                    .then_inc(S["elu"], 1)

            run_slots(dve, B, 2, [
                (stats_x, 0), (mask_kv, 3), (clamp, 2), (elu, 2),
                (divide, 3), (stats_x1, 4)])

            done = 0

            def chain(ins):
                nonlocal done
                done += 1
                ins.then_inc(routed, 1)
                dve.wait_ge(routed, done)

            def over_tiles(row):
                return row.unsqueeze(2).to_broadcast([P, E, NT])

            def over_experts(row):
                return row.unsqueeze(1).to_broadcast([P, E, NT])

            dve.wait_ge(S["lg"], B)
            left = LG
            for c in range(K):
                chain(dve.tensor_reduce(top[c][:], left[:].rearrange("p e t -> p t e"), AX.X, ALU.max))
                if c == 1:
                    dve.tensor_tensor(GD[:], top[1][:], top[0][:], ALU.subtract).then_inc(gates_diff, 1)
                chain(dve.tensor_tensor(hit[:], left[:], over_experts(top[c][:]), ALU.is_equal))
                chain(dve.tensor_tensor(numb[:], hit[:], over_tiles(iota_e[:]), ALU.mult))
                chain(dve.tensor_reduce(which[:], numb[:].rearrange("p e t -> p t e"), AX.X, ALU.max))
                chain(dve.tensor_tensor(OH[:, c], numb[:], over_experts(which[:]), ALU.is_equal))
                if c == 0:
                    chain(dve.scalar_tensor_tensor(lg[:], OH[:, 0], -3.0e38, LG[:], ALU.mult, ALU.add))
                    left = lg
            dve.tensor_tensor(CNT[:], OH[:, 0], OH[:, 1], ALU.add).then_inc(counts_made, 1)
            dve.wait_ge(counts_ps, 1)
            chain(dve.tensor_copy(TOT[:], bank[1][:, 0:E * NT]))
            chain(dve.tensor_tensor_scan(CUM[:], ONEf[:], TOT[:], 0.0, ALU.mult, ALU.add))
            chain(dve.tensor_tensor(CUM[:], CUM[:], TOT[:], ALU.subtract))
            chain(dve.tensor_tensor(BASE[:], bank[0][:, 0:E * NT], CUM[:], ALU.add))
            chain(dve.tensor_tensor(PRD[:].rearrange("p c e t -> p c (e t)"),
                                    OH[:].rearrange("p c e t -> p c (e t)"),
                                    BASE[:].unsqueeze(1).to_broadcast([P, K, E * NT]), ALU.mult))
            chain(dve.tensor_reduce(POSf[:], PRD[:].rearrange("p c e t -> p c t e"), AX.X, ALU.add))
            chain(dve.tensor_copy(POSu[:], POSf[:].rearrange("p c t -> p (c t)")))
            dve.tensor_scalar(HIu[:], POSu[:], P.bit_length() - 1, None, ALU.logical_shift_right)
            chain(dve.tensor_scalar(LOu[:], POSu[:], P - 1, None, ALU.bitwise_and))
            dve.tensor_copy(HIf[:], HIu[:])
            chain(dve.tensor_copy(LOf[:], LOu[:]))
            for q in range(CH):
                cols = slice(q * CW, (q + 1) * CW)
                dve.tensor_tensor(OHHI[:, cols, :], iota_lo[:, 0:NS].unsqueeze(1).to_broadcast([P, CW, NS]),
                                  HIf[:, cols].unsqueeze(2).to_broadcast([P, CW, NS]), ALU.is_equal)\
                    .then_inc(hi_made, 1)
                dve.tensor_tensor(OHLO[:, cols, :], iota_lo[:].unsqueeze(1).to_broadcast([P, CW, P]),
                                  LOf[:, cols].unsqueeze(2).to_broadcast([P, CW, P]), ALU.is_equal)\
                    .then_inc(lo_made, 1)
            dve.scalar_tensor_tensor(EIDX[:], LOf[:], float(NS), HIf[:], ALU.mult, ALU.add).then_inc(eidx_made, 1)
            dve.wait_ge(ids_ps, 1)
            chain(dve.tensor_copy(SIDXf[:], bank[2][:, 0:NS]))
            dve.scalar_tensor_tensor(SIDX[:], bank[2][:, NS:2 * NS], float(NT), SIDXf[:], ALU.mult, ALU.add)\
                .then_inc(ids_ready, 1)
            dve.wait_ge(gates_exp, 1)
            chain(dve.tensor_scalar(GS[:], GE[:], 1.0, None, ALU.add))
            chain(dve.reciprocal(GW[:, 0, :], GS[:]))
            chain(dve.tensor_tensor(GW[:, 1, :], GE[:], GW[:, 0, :], ALU.mult))
            gates = GW[:].rearrange("p c t -> p (c t)")
            for part in range(2):
                chain(dve.tensor_copy(gate_part[part][:], gates if part == 0 else gate_rest[:]))
                chain(dve.tensor_tensor(gate_rest[:], gates if part == 0 else gate_rest[:], gate_part[part][:],
                                        ALU.subtract))
            chain(dve.tensor_copy(gate_part[2][:], gate_rest[:]))

            def weigh_onehots(st):
                if st.steady or st.t >= len(GATE_CHUNKS):
                    return
                for q in GATE_CHUNKS[st.t]:
                    cols = slice(q * CW, (q + 1) * CW)
                    for part in range(3):
                        dve.tensor_tensor(OHW[:, cols, part * NS:(part + 1) * NS], OHHI[:, cols, :],
                                          gate_part[part][:, cols].unsqueeze(2).to_broadcast([P, CW, NS]),
                                          ALU.mult).then_inc(weighted, 1)

            def keep_gates(st):
                if not st.steady and st.t == 0:
                    dve.wait_ge(gates_ps, 1)
                    chain(dve.tensor_copy(gate_sum[:], bank[7][:, 2 * NS:3 * NS]))
                    chain(dve.tensor_tensor(gate_sum[:], bank[7][:, NS:2 * NS], gate_sum[:], ALU.add))
                    dve.tensor_tensor(WS[:], bank[7][:, 0:NS], gate_sum[:], ALU.add).then_inc(gates_ready, 1)
                    dve.wait_ge(gates_ready, 1)

            def rest_weights(st):
                if st.k % 2 == 0:
                    half = (st.k // 2) % 2
                    dve.wait_ge(F["whi"], st.pair + 1)
                    dve.tensor_tensor(W1lo[half][:], W1s[half][:], W1hi[half][:].bitcast(F32), ALU.subtract)\
                        .then_inc(F["wlo"], 1)

            def rest_x(st):
                i = st.k % 2
                dve.wait_ge(F["xhi"], st.t + 1)
                if has_prior(st, 2):
                    dve.wait_ge(F["h_ps"], FB * st.t - FB)
                dve.tensor_tensor(xlo[i][:], bank[i], xhi[i][:].bitcast(F32), ALU.subtract)\
                    .then_inc(F["xlo"], 1)

            def weigh_rows(st):
                i = st.k % 2
                dve.wait_ge(F["out_ps"], st.t + 1)
                if has_prior(st, 2):
                    dve.wait_ge(eo_stored[i], 16 * st.pair)
                dve.tensor_tensor(eo[i][:], bank[6 + i].rearrange("p (n d) -> p n d", n=G),
                                  WS[:, bass.ts(st.t, G)].unsqueeze(2).to_broadcast([P, G, D]), ALU.mult)\
                    .then_inc(F["eo"], 1)

            run_slots(dve, NG, 4, [
                (weigh_onehots, 0), (rest_weights, 0), (rest_x, 0), (keep_gates, 2),
                (weigh_rows, 2)])

            def stats_x2(st):
                wait_alone(dve, e1_in[st.k % 2], 16 * TPB * (st.pair + 1))
                norm_stats(st, N3, norm1, lambda n: x2[st.k][:, n, :])

            def maxima(st):
                i = st.k % 2
                dve.wait_ge(C["proj"], st.t + 1)
                dve.wait_ge(C["v"], st.t + 1)
                q_ = psum[:, 1:3, 0:D].rearrange("p n (h d) -> p n h d", d=HD)
                k_ = psum[:, 1:3, D:2 * D].rearrange("p n (h d) -> p n h d", d=HD)
                dve.tensor_reduce(qmax[i][:], q_, AX.X, ALU.max).then_inc(C["qmax"], 1)
                dve.tensor_reduce(kmax[i][:], k_.rearrange("p n h d -> p n d h"), AX.X, ALU.max)\
                    .then_inc(C["kmax"], 1)
                dve.wait_ge(C["qmax"], st.t + 1)
                if has_prior(st, 2):
                    dve.wait_ge(C["qke"], st.t - 1)
                dve.tensor_tensor(qk[i][:, :, 0:D].rearrange("p n (h d) -> p n h d", d=HD), q_,
                                  qmax[i][:].unsqueeze(3).to_broadcast([P, TPB, HEADS, HD]),
                                  ALU.subtract).then_inc(C["qk0"], 1)
                dve.wait_ge(C["kmax"], st.t + 1)
                dve.tensor_tensor(qk[i][:, :, D:].rearrange("p n (h d) -> p n h d", d=HD), k_,
                                  kmax[i][:].unsqueeze(2).to_broadcast([P, TPB, HEADS, HD]),
                                  ALU.subtract).then_inc(C["qk"], 1)

            def products_kv(st):
                dve.wait_ge(C["qke"], st.t + 1)
                if has_prior(st, 2):
                    dve.wait_ge(C["tv_ps"], st.t - 1)
                dve.tensor_tensor(*outer_kv(st.k % 2, 0), ALU.mult).then_inc(C["p1"], 1)

            def sums(st):
                i = st.k % 2
                dve.wait_ge(C["qke"], st.t + 1)
                eq_ = qke[i][:, :, 0:D].rearrange("p n (h d) -> p n h d", d=HD)
                ek_ = qke[i][:, :, D:].rearrange("p n (h d) -> p n d h", d=HD)
                dve.tensor_reduce(qsum[i][:], eq_, AX.X, ALU.add).then_inc(C["qsum"], 1)
                dve.tensor_reduce(ksum[i][:], ek_, AX.X, ALU.add).then_inc(C["ksum"], 1)
                dve.wait_ge(C["qsum"], st.t + 1)
                dve.reciprocal(rqs[i][:], qsum[i][:]).then_inc(C["rqs"], 1)
                dve.wait_ge(C["ksum"], st.t + 1)
                dve.reciprocal(rks[i][:], ksum[i][:]).then_inc(C["rks"], 1)
                dve.wait_ge(C["rqs"], st.t + 1)
                dve.tensor_tensor(qn[i][:].rearrange("p n (h d) -> p n h d", d=HD), eq_,
                                  rqs[i][:].unsqueeze(3).to_broadcast([P, TPB, HEADS, HD]), ALU.mult)\
                    .then_inc(C["qn"], 1)

            def mean_v(st):
                i = st.k % 2
                if has_prior(st, 2):
                    dve.wait_ge(C["p2_0"], st.t - 1)
                    dve.wait_ge(C["p2"], st.t - 1)
                dve.wait_ge(C["rks"], st.t + 1)
                dve.wait_ge(C["tv_ps"], st.t + 1)
                dve.tensor_tensor(
                    tv[i][:].rearrange("p n (d e) -> p n d e", d=HD),
                    bank[3][:, 0:TPB * HD * HD].rearrange("p (n d e) -> p n d e", n=TPB, d=HD),
                    rks[i][:].unsqueeze(3).to_broadcast([P, TPB, HD, HD]), ALU.mult).then_inc(C["tv"], 1)

            def products_q(st, n):
                i = st.k % 2
                dve.wait_ge(C["tv"], st.t + 1)
                dve.wait_ge(C["qn"], st.t + 1)
                if has_prior(st, 1):
                    dve.wait_ge(C["out_ps" if n else "out0_ps"], st.t)
                dve.tensor_tensor(
                    p2[n][:].rearrange("p (d h e) -> p d h e", h=HEADS, d=HD),
                    qn[i][:, n, :].rearrange("p (h d) -> p d h", d=HD).unsqueeze(3)
                    .to_broadcast([P, HD, HEADS, HD]),
                    tv[i][:, n, :].rearrange("p (d e) -> p d e", d=HD).unsqueeze(2)
                    .to_broadcast([P, HD, HEADS, HD]), ALU.mult).then_inc(C["p2" if n else "p2_0"], 1)

            def products_q0(st):
                products_q(st, 0)

            def products_q1(st):
                products_q(st, 1)

            def stats_x3(st):
                wait_alone(dve, C["x3"], st.t + 1)
                norm_stats(st, N4, norm2, lambda n: x3[st.k % 2][:, n, :])

            def finish(st):
                i = st.k % 2
                dve.wait_ge(C["v_ps"], st.t + 1)
                dve.scalar_tensor_tensor(rkv[i][:], th[i][:], 1.0,
                                         bank[7][:, 0:TPB * D].rearrange("p (n d) -> p n d", n=TPB),
                                         ALU.add, ALU.mult).then_inc(C["rkv"], 1)
                dve.wait_ge(C["rkv"], st.t + 1)
                if has_prior(st, 2):
                    dve.wait_ge(out_stored[i], 16 * st.pair)
                dve.tensor_tensor(fin[i][:], rkv[i][:], x3[i][:], ALU.add).then_inc(C["fin"], 1)

            run_slots(dve, B, 4, [
                (products_q1, 2), (products_q0, 2), (maxima, 1), (stats_x2, 0),
                (finish, 4), (products_kv, 1), (sums, 1), (stats_x3, 2), (mean_v, 1)])

        @block.tensor
        def _(pe):
            def transposes(st, sems, ready, done, dst, src):
                pe.wait_ge(sems[ready], st.t + 1)
                for n in range(TPB):
                    ins = pe.transpose(dst[:, n * P:(n + 1) * P], src(n), ident[:])
                ins.then_inc(sems[done], 1)

            pe.wait_ge(weights_in, 32)
            pe.wait_ge(consts_made, consts)

            def turn_xn(st):
                if has_prior(st, 1):
                    pe.wait_ge(S["xnT"], st.t)
                transposes(st, S, "xn", "xnT_ps", bank[0], lambda n: xn[st.k % 2][:, n, :])

            def sum_kv(st):
                i = st.k % 2
                pe.wait_ge(S["elu0"], st.t + 1)
                if has_prior(st, 1):
                    pe.wait_ge(S["kv"], st.t)
                for n in range(TPB):
                    ins = pe.matmul(bank[3][:, 0:D + 1], kt[i][:, n, :], vt[i][:, n, :],
                                    start=(n == 0), stop=(n == TPB - 1))
                ins.then_inc(S["kv_ps"], 1)

            def turn_xm(st):
                if has_prior(st, 1):
                    pe.wait_ge(S["lg"], st.t)
                transposes(st, S, "xm", "xmT_ps", bank[7], lambda n: xm[st.k % 2][:, n, :])

            def project(st):
                i = st.k % 2
                pe.wait_ge(S["xnT"], st.t + 1)
                if has_prior(st, 1):
                    pe.wait_ge(S["elu"], st.t)
                pe.matmul(bank[1][:, 0:T], W[:, cQ:cQ + D], xnT[i][:], start=True, stop=True)
                for n in range(TPB):
                    ins = pe.matmul(bank[2][:, 2 * D * n:2 * D * (n + 1)], xnT[i][:, n * P:(n + 1) * P],
                                    W[:, cKV:cKV + 2 * D], start=True, stop=True)
                ins.then_inc(S["proj"], 1)

            def project_out(st):
                i = st.k % 2
                pe.wait_ge(S["attT"], st.t + 1)
                if has_prior(st, 1):
                    pe.wait_ge(S["x1"], st.t)
                for n in range(TPB):
                    dst = bank[6][:, n * D:(n + 1) * D]
                    pe.matmul(dst, ident[:], X[:, st.t * TPB + n, :], start=True, stop=False)
                    ins = pe.matmul(dst, attT[i][:, n * P:(n + 1) * P], W[:, cO:cO + D], start=False, stop=True)
                ins.then_inc(S["wo"], 1)

            def attend(st):
                i = st.k % 2
                pe.wait_ge(S["kv"], st.t + 1)
                if has_prior(st, 1):
                    pe.wait_ge(S["att"], st.t)
                w = D + HEADS
                for n in range(TPB):
                    ins = pe.matmul(bank[4][:, n * w:(n + 1) * w], qT[i][:, n * P:(n + 1) * P], kv[i][:],
                                    start=True, stop=True)
                ins.then_inc(S["num"], 1)

            def route(st):
                i = st.k % 2
                pe.wait_ge(S["xmT"], st.t + 1)
                for n in range(TPB):
                    ins = pe.matmul(bank[7][:, T + n * E:T + (n + 1) * E], xmT[i][:, n * P:(n + 1) * P],
                                    W[:, cR:cR + E], start=True, stop=True)
                ins.then_inc(S["logits"], 1)

            def turn_att(st):
                if has_prior(st, 1):
                    pe.wait_ge(S["attT"], st.t)
                transposes(st, S, "att", "attT_ps", bank[5], lambda n: att[st.k % 2][:, n, :])

            run_slots(pe, B, 2, [
                (project, 1), (sum_kv, 2), (turn_att, 3), (turn_xm, 5),
                (turn_xn, 0), (attend, 2), (project_out, 3), (route, 5)])

            pe.wait_ge(counts_made, 1)
            cnt = CNT[:].rearrange("p e t -> p (e t)")
            pe.matmul(bank[1][:, 0:E * NT], ones[:], cnt, start=True, stop=True)
            pe.matmul(bank[0][:, 0:E * NT], before[:], cnt, start=True, stop=True).then_inc(counts_ps, 1)
            for j in range(K * NT):
                if j % CW == 0:
                    for made in (lo_made, by_tile, by_part):
                        pe.wait_ge(made, j // CW + 1)
                ins = pe.matmul(bank[2][:, 0:2 * NS], OHLO[:, j, :], OHID[:, j, :],
                                start=(j == 0), stop=(j == K * NT - 1))
            ins.then_inc(ids_ps, 1)

            def place_gates(st):
                if st.steady or st.t >= len(GATE_CHUNKS):
                    return
                for q in GATE_CHUNKS[st.t]:
                    pe.wait_ge(weighted, 3 * q + 3)
                    for j in range(q * CW, (q + 1) * CW):
                        ins = pe.matmul(bank[7][:, 0:3 * NS], OHLO[:, j, :], OHW[:, j, :],
                                        start=(j == 0), stop=(j == K * NT - 1))
                if q == CH - 1:
                    ins.then_inc(gates_ps, 1)

            def turn_rows(st):
                i = st.k % 2
                pe.wait_ge(xg_in[i], 16 * G * (st.pair + 1))
                if has_prior(st, 2):
                    pe.wait_ge(F["xlo"], st.t - 1)
                for n in range(G):
                    ins = pe.transpose(bank[i][:, n * P:(n + 1) * P], xg[i][:, n, :], ident[:])
                ins.then_inc(F["xgT_ps"], 1)

            def hidden(st):
                i, half = st.k % 2, (st.k // 2) % 2
                pe.wait_ge(F["xlo"], st.t + 1)
                if st.k % 2 == 0:
                    pe.wait_ge(F["wlo"], st.pair + 1)
                for f in range(FB):
                    if has_prior(st, 1):
                        pe.wait_ge(F["h"], FB * st.t - FB + f + 1)
                    hi, lo = (w[half][:, f * P:(f + 1) * P] for w in (W1hi, W1lo))
                    pe.matmul(bank[2 + f], hi, xhi[i][:], start=True, stop=False)
                    pe.matmul(bank[2 + f], hi, xlo[i][:], start=False, stop=False)
                    pe.matmul(bank[2 + f], lo, xhi[i][:], start=False, stop=True).then_inc(F["h_ps"], 1)

            def expert_rows(st):
                i, half = st.k % 2, (st.k // 2) % 2
                pe.wait_ge(F["h"], FB * st.t + FB)
                if has_prior(st, 2):
                    pe.wait_ge(F["eo"], st.t - 1)
                elif st.t == 1:
                    pe.wait_ge(gates_ready, 1)
                for n in range(G):
                    for f in range(FB):
                        ins = pe.matmul(bank[6 + i][:, n * D:(n + 1) * D], h[i][:, f, n * P:(n + 1) * P],
                                        W2s[half][:, f * D:(f + 1) * D], start=(f == 0), stop=(f == FB - 1))
                ins.then_inc(F["out_ps"], 1)

            run_slots(pe, NG, 4, [
                (turn_rows, 0), (place_gates, 0), (hidden, 1), (expert_rows, 2)])

            pe.wait_ge(C["heads"], 6)
            pe.wait_ge(F["eo"], NG)

            def turn_y3(st):
                if has_prior(st, 1):
                    pe.wait_ge(C["y3T"], st.t)
                transposes(st, C, "y3", "y3T_ps", bank[0], lambda n: y3[st.k % 2][:, n, :])

            def project_qkv(st):
                i = st.k % 2
                pe.wait_ge(C["y3T"], st.t + 1)
                if has_prior(st, 1):
                    pe.wait_ge(C["qk"], st.t)
                for n in range(TPB):
                    ins = pe.matmul(bank[1 + n][:, 0:3 * D], y3T[i][:, n * P:(n + 1) * P],
                                    W[:, cQKV:cQKV + 3 * D], start=True, stop=True)
                ins.then_inc(C["proj"], 1)

            def sum_heads(st):
                i = st.k % 2
                pe.wait_ge(C["p1"], st.t + 1)
                pe.wait_ge(C["p1_pool"], st.t + 1)
                if has_prior(st, 1):
                    pe.wait_ge(C["tv"], st.t)
                w = HD * HD
                for c in range(HEADS):
                    ins = pe.matmul(bank[3][:, 0:TPB * w].rearrange("p (n w) -> p n w", n=TPB), ident[:],
                                    p1[i][:, :, c * w:(c + 1) * w], start=(c == 0), stop=(c == HEADS - 1))
                ins.then_inc(C["tv_ps"], 1)

            def sum_channels(st, n):
                dst = bank[4][:, n * D:(n + 1) * D]
                if has_prior(st, 1):
                    pe.wait_ge(C["x3"], st.t)
                pe.wait_ge(C["p2" if n else "p2_0"], st.t + 1)
                pe.matmul(dst, ident[:], x2[st.k][:, n, :], start=True, stop=False)
                for c in range(HD):
                    ins = pe.matmul(dst, ident[:], p2[n][:, c * D:(c + 1) * D], start=False, stop=(c == HD - 1))
                ins.then_inc(C["out_ps" if n else "out0_ps"], 1)

            def sum_channels0(st):
                sum_channels(st, 0)

            def sum_channels1(st):
                sum_channels(st, 1)

            def turn_y4(st):
                if has_prior(st, 1):
                    pe.wait_ge(C["y4T"], st.t)
                transposes(st, C, "y4", "y4T_ps", bank[5], lambda n: y4[st.k % 2][:, n, :])

            def mix_rk(st):
                i = st.k % 2
                pe.wait_ge(C["y4T"], st.t + 1)
                if has_prior(st, 1):
                    pe.wait_ge(C["ka"], st.t)
                pe.matmul(bank[6][:, T:], W[:, cFK:cFK + D], y4T[i][:, 1:], start=True, stop=False)
                pe.matmul(bank[6][:, T:], WP[:, D:2 * D], y4T[i][:, 0:T], start=False, stop=True)
                for n in range(TPB):
                    dst = bank[6][:, n * D:(n + 1) * D]
                    pe.matmul(dst, y4T[i][:, 1 + n * P:1 + (n + 1) * P], W[:, cFR:cFR + D],
                              start=True, stop=False)
                    ins = pe.matmul(dst, y4T[i][:, n * P:(n + 1) * P], WP[:, 0:D], start=False, stop=True)
                ins.then_inc(C["rk_ps"], 1)

            def mix_values(st):
                i = st.k % 2
                pe.wait_ge(C["ka"], st.t + 1)
                if has_prior(st, 1):
                    pe.wait_ge(C["rkv"], st.t)
                for n in range(TPB):
                    ins = pe.matmul(bank[7][:, n * D:(n + 1) * D], ka[i][:, n * P:(n + 1) * P],
                                    W[:, cFV:cFV + D], start=True, stop=True)
                ins.then_inc(C["v_ps"], 1)

            run_slots(pe, B, 4, [
                (project_qkv, 1), (turn_y4, 3), (sum_channels1, 2), (sum_channels0, 2),
                (mix_rk, 3), (turn_y3, 0), (sum_heads, 1), (mix_values, 3)])


def kernel(**inputs):
    import numpy as np
    import concourse.bacc as bacc
    from concourse.bass_utils import run_bass_kernel_spmd

    x = np.asarray(inputs["L0_attn_x"])
    tiles = x.shape[0] * x.shape[1] // P

    def t(name):
        return np.asarray(inputs[name]).T

    arrays = {
        "x": np.ascontiguousarray(x.reshape(tiles, P, D).transpose(1, 0, 2)),
        "wa": np.ascontiguousarray(np.concatenate(
            [t("L0_attn_w_qkv"), t("L0_attn_w_out"), t("L0_ffn_Wr"), t("L1_attn_W_Q"), t("L1_attn_W_K"),
             t("L1_attn_W_V"), t("L1_ffn_W_r"), t("L1_ffn_W_k"), t("L1_ffn_W_v")], axis=1)),
        "w1": np.ascontiguousarray(inputs["L0_ffn_W1"]),
        "w2": np.ascontiguousarray(np.asarray(inputs["L0_ffn_W2"]).reshape(8, 4, P, D).transpose(0, 2, 1, 3)),
        "mu": np.ascontiguousarray(np.stack([inputs["L1_ffn_mu_r"], inputs["L1_ffn_mu_k"]], axis=1)),
    }
    nc = bacc.Bacc("TRN2", target_bir_lowering=False, num_devices=1)
    args = [nc.dram_tensor(name, a.shape, F32, kind="ExternalInput").ap() for name, a in arrays.items()]
    out = nc.dram_tensor("out", (P, tiles, D), F32, kind="ExternalOutput").ap()
    build(nc, *args, out)
    r = run_bass_kernel_spmd(nc, [arrays], core_ids=[0])
    return r.results[0]["out"].transpose(1, 0, 2).reshape(x.shape)
```

```python
from collections import namedtuple
from contextlib import ExitStack

import concourse.bass as bass
from concourse import mybir

F32 = mybir.dt.float32
BF16 = mybir.dt.bfloat16
F32R = mybir.dt.float32r
U32 = mybir.dt.uint32
ALU = mybir.AluOpType
ACT = mybir.ActivationFunctionType
AX = mybir.AxisListType

P = 128
D = 128
HEADS = 16
HD = D // HEADS
EPS = 1e-5

Slot = namedtuple("Slot", "m k unroll steady count")
Step = namedtuple("Step", "t pair quad k steady")


def run_slots(eng, count, unroll, stages):
    last_lag = max(lag for _, lag in stages)

    def body(slot):
        for stage, lag in stages:
            if st := item(slot, lag):
                stage(st)

    peeled = -(-(last_lag + 2) // unroll)
    for m in range(peeled):
        for k in range(unroll):
            body(Slot(m, k, unroll, False, count))
    with eng.Fori(peeled, count // unroll) as m:
        for k in range(unroll):
            body(Slot(m, k, unroll, True, count))
    for s in range(count, count + last_lag):
        body(Slot(s // unroll, s % unroll, unroll, False, count))


def item(slot, lag):
    j = slot.k - lag
    t = slot.unroll * slot.m + j
    if not slot.steady and not 0 <= t < slot.count:
        return None
    return Step(t, (slot.unroll // 2) * slot.m + j // 2, slot.m + j // 4, j % slot.unroll, slot.steady)


def has_prior(st, n):
    return st.steady or st.t >= n


def build(nc, x, wa, w1, w2, mu, out):
    B, T = 16, 256
    TPB = T // P
    N = B * T
    NT = N // P
    E, FF = w1.shape[0], w1.shape[2]
    FB = FF // P
    K = 2
    NS = N * K // P
    G = 4
    NG = NS // G
    GPC = NG // E
    assert GPC == 2 and TPB == 2

    cQ, cKV, cO, cR = 0, D, 3 * D, 4 * D
    cQKV = cR + E
    cFR = cQKV + 3 * D
    cFK, cFV = cFR + D, cFR + 2 * D
    cEnd = cFR + 3 * D
    CH = 4
    CW = K * NT // CH
    FOLD = (HD // 2, HD // 4)
    GATE_CHUNKS = ((0, 1), (2,), (3,))
    assert wa.shape == (P, cEnd)

    xn_dram = nc.dram_tensor("xn_dram", (P * NT, D), F32).ap()
    eo_dram = nc.dram_tensor("eo_dram", (P * NS, D), F32).ap()
    xn_rows = xn_dram.rearrange("(p t) d -> p t d", p=P)
    eo_rows = eo_dram.rearrange("(p t) d -> p t d", p=P)

    with ExitStack() as ctx:
        def sb(name, shape, dt=F32):
            return ctx.enter_context(nc.sbuf_tensor(name, shape, dt))

        def two(name, shape, dt=F32):
            return [sb(f"{name}{i}", shape, dt) for i in range(2)]

        def sem(name):
            return ctx.enter_context(nc.semaphore(name))

        psum = ctx.enter_context(nc.psum_tensor("psum", [P, 8, 512], F32))
        bank = [psum[:, i, :] for i in range(8)]

        W = sb("W", [P, cEnd])
        WP = sb("WP", [P, 2 * D])
        MU = sb("MU", [P, 2])
        OMM = sb("OMM", [P, 2])
        ident = sb("ident", [P, P])
        block_mask = sb("block_mask", [P, D + HEADS])
        neg_half = sb("neg_half", [P, TPB])
        iota_e = sb("iota_e", [P, E])
        before = sb("before", [P, P], BF16)
        ones = sb("ones", [P, P], BF16)
        iota_lo = sb("iota_lo", [P, P])
        iota_tile = sb("iota_tile", [P, NT])
        iota_part = sb("iota_part", [P, 1])
        y4T = two("y4T", [P, 1 + T])
        vt = two("vt", [P, TPB, D + 1])
        ONEf = sb("ONEf", [P, E * NT])

        X = sb("X", [P, NT, D])
        LG = sb("LG", [P, E, NT])
        EIDX = sb("EIDX", [P, K * NT], U32)
        SIDX = sb("SIDX", [P, NS], U32)
        WS = sb("WS", [P, NS])
        SIDX_col = two("SIDX_col", [P, G], U32)
        EIDX_col = [sb(f"EIDX_col{i}", [P, TPB * K], U32) for i in range(4)]

        xm = two("xm", [P, TPB, D])

        def norm_buffers(i):
            return dict(stats=two(f"stats{i}", [P, TPB, 6]), mv=two(f"mv{i}", [P, TPB, 2]),
                        veps=two(f"veps{i}", [P, TPB]), nmean=two(f"nmean{i}", [P, TPB]),
                        rstd=two(f"rstd{i}", [P, TPB]), nmr=two(f"nmr{i}", [P, TPB]))

        norm1, norm2 = norm_buffers(1), norm_buffers(2)

        W1s = two("W1s", [P, FF])
        W2s = two("W2s", [P, FB * D])
        W1hi, W1lo = two("W1hi", [P, FF], F32R), two("W1lo", [P, FF], F32R)
        xhi, xlo = two("xhi", [P, G * P], F32R), two("xlo", [P, G * P], F32R)
        h = two("h", [P, FB, G * P])
        xg = two("xg", [P, G, D])
        eo = two("eo", [P, G, D])

        outer, ctx_a = ctx, ExitStack()
        ctx = ctx_a
        xn = two("xn", [P, TPB, D])
        xnT = two("xnT", [P, T])
        eq = two("eq", [P, T + TPB * D])
        em = two("em", [P, T + TPB * D])
        qT = two("qT", [P, T])
        kt = two("kt", [P, TPB, D])
        kv = two("kv", [P, D + HEADS])
        den = two("den", [P, TPB, HEADS])
        rden = two("rden", [P, TPB, HEADS])
        att = two("att", [P, TPB, D])
        attT = two("attT", [P, T])
        xmT = two("xmT", [P, T])
        ctx_a.close()

        ctx = ctx_r = ExitStack()
        lg = sb("lg", [P, E, NT])
        top = [sb(f"top{c}", [P, NT]) for c in range(K)]
        hit = sb("hit", [P, E, NT])
        numb = sb("numb", [P, E, NT])
        which = sb("which", [P, NT])
        OH = sb("OH", [P, K, E, NT])
        CNT = sb("CNT", [P, E, NT], BF16)
        CUM = sb("CUM", [P, E * NT])
        BASE = sb("BASE", [P, E * NT])
        PRD = sb("PRD", [P, K, E, NT])
        POSf = sb("POSf", [P, K, NT])
        POSu = sb("POSu", [P, K * NT], U32)
        LOu = sb("LOu", [P, K * NT], U32)
        HIu = sb("HIu", [P, K * NT], U32)
        LOf = sb("LOf", [P, K * NT])
        HIf = sb("HIf", [P, K * NT])
        GD = sb("GD", [P, NT])
        GE = sb("GE", [P, NT])
        GS = sb("GS", [P, NT])
        GW = sb("GW", [P, K, NT])
        OHLO = sb("OHLO", [P, K * NT, P], BF16)
        OHHI = sb("OHHI", [P, K * NT, NS], BF16)
        OHID = sb("OHID", [P, K * NT, 2 * NS], BF16)
        OHW = sb("OHW", [P, K * NT, 3 * NS], BF16)
        gate_part = [sb(f"gate_part{i}", [P, K * NT], BF16) for i in range(3)]
        gate_rest = sb("gate_rest", [P, K * NT])
        gate_sum = sb("gate_sum", [P, NS])
        SIDXf = sb("SIDXf", [P, NS])
        ctx_r.close()

        ctx = ctx_c = ExitStack()
        x2 = [sb(f"x2_{i}", [P, TPB, D]) for i in range(4)]
        y3 = two("y3", [P, TPB, D])
        y3T = two("y3T", [P, T])
        qmax = two("qmax", [P, TPB, HEADS])
        kmax = two("kmax", [P, TPB, HD])
        qk = two("qk", [P, TPB, 2 * D])
        qke = two("qke", [P, TPB, 2 * D])
        vc = two("vc", [P, TPB, D])
        qsum = two("qsum", [P, TPB, HEADS])
        ksum = two("ksum", [P, TPB, HD])
        rqs = two("rqs", [P, TPB, HEADS])
        rks = two("rks", [P, TPB, HD])
        qn = two("qn", [P, TPB, D])
        p1 = two("p1", [P, TPB, HEADS * HD * HD])
        tv = two("tv", [P, TPB, HD * HD])
        p2 = two("p2", [P, HD * HEADS * HD])
        x3 = [sb(f"x3_{i}", [P, TPB, D]) for i in range(4)]
        sum4 = two("sum4", [P, TPB])
        square_sum4 = two("square_sum4", [P, TPB])
        sum3 = two("sum3", [P, TPB])
        square_sum3 = two("square_sum3", [P, TPB])
        copy3 = two("copy3", [P, TPB, D])
        scratch3, scratch4 = two("scratch3_", [P, TPB, D]), two("scratch4_", [P, TPB, D])
        y4 = two("y4", [P, TPB, D])
        kr = two("kr", [P, T])
        ka = two("ka", [P, T])
        th = two("th", [P, TPB, D])
        rkv = two("rkv", [P, TPB, D])
        fin = two("fin", [P, TPB, D])
        ctx_c.close()
        ctx = outer

        weights_in = sem("weights_in")
        consts_made = sem("consts_made")
        x_in = [sem(f"x_in{i}") for i in range(2)]
        norm_names = "stats aggr mv veps nmean rstd nmr"
        S = {n: sem("a_" + n) for n in """xn0 xn xnT_ps xnT proj eq0 eq v em elu0 elu kv_ps kv0 kv num den rden att
            attT_ps attT wo x1 xm0 xm xmT_ps xmT logits lg""".split()}
        N1 = {n: sem("a1_" + n) for n in norm_names.split()}
        N2 = {n: sem("a2_" + n) for n in norm_names.split()}
        norm_names = "sum0 sum squares0 squares veps nmean rstd nmr"
        N3 = {n: sem("c1_" + n) for n in norm_names.split()}
        N4 = {n: sem("c2_" + n) for n in norm_names.split()}
        xn_stored = [sem(f"xn_stored{i}") for i in range(2)]
        routed = sem("routed")
        counts_made = sem("counts_made")
        counts_ps = sem("counts_ps")
        gates_diff = sem("gates_diff")
        gates_exp = sem("gates_exp")
        hi_made = sem("hi_made")
        lo_made = sem("lo_made")
        by_tile = sem("by_tile")
        by_part = sem("by_part")
        eidx_made = sem("eidx_made")
        ids_ps = sem("ids_ps")
        ids_ready = sem("ids_ready")
        weighted = sem("weighted")
        gates_ps = sem("gates_ps")
        gates_ready = sem("gates_ready")
        w_in = [sem(f"w_in{i}") for i in range(2)]
        F = {n: sem("f_" + n) for n in """idx xgT_ps xhi xlo whi wlo h_ps h out_ps eo""".split()}
        xg_in = [sem(f"xg_in{i}") for i in range(2)]
        eo_stored = [sem(f"eo_stored{i}") for i in range(2)]
        x1_in = [sem(f"x1_in{i}") for i in range(4)]
        e0_in = [sem(f"e0_in{i}") for i in range(2)]
        e1_in = [sem(f"e1_in{i}") for i in range(2)]
        C = {n: sem("c_" + n) for n in """heads idx y30 y3 y3T_ps y3T proj qmax kmax qk0 qk v qke p1 p1_pool p1_sum ksum qsum
            rks rqs qn tv_ps tv p2_0 p2_0_sum p2_sum p2 out0_ps out_ps y40 y4 y4T_ps y4T rk_ps relu th ka v_ps rkv fin""".split()}
        out_stored = [sem(f"out_stored{i}") for i in range(2)]

        consts = 20

        def wait_alone(eng, sem_, value):
            value = value if isinstance(value, int) else eng.to_reg(value)
            eng.wait_ge(consts_made, 1)
            eng.wait_ge(sem_, value)

        def outer_kv(i, n):
            return (p1[i][:, n, :].rearrange("p (h d e) -> p h d e", h=HEADS, d=HD),
                    qke[i][:, n, D:].rearrange("p (h d) -> p h d", d=HD).unsqueeze(3)
                    .to_broadcast([P, HEADS, HD, HD]),
                    vc[i][:, n, :].rearrange("p (h e) -> p h e", e=HD).unsqueeze(2)
                    .to_broadcast([P, HEADS, HD, HD]))

        block = ctx.enter_context(nc.Block())

        @block.sync
        def _(sp):
            def load_x(st):
                if has_prior(st, 2):
                    wait_alone(sp, x_in[st.k % 2], 16 * st.pair)
                sp.dma_start(X[:, bass.ts(st.t, TPB), :], x[:, bass.ts(st.t, TPB), :])\
                    .then_inc(x_in[st.k % 2], 16)
                if not st.steady and st.t == 0:
                    sp.dma_start(W[:], wa).then_inc(weights_in, 16)
                    sp.dma_start(MU[:], mu).then_inc(weights_in, 16)

            def store_xn(st):
                if has_prior(st, 2):
                    wait_alone(sp, xn_stored[st.k % 2], 16 * st.pair)
                wait_alone(sp, S["xm"], st.t + 1)
                sp.dma_start(xn_rows[:, bass.ts(st.t, TPB), :], xm[st.k % 2][:])\
                    .then_inc(xn_stored[st.k % 2], 16)

            run_slots(sp, B, 2, [(load_x, 0), (store_xn, 8)])

            def load_weights(st):
                if st.k % 2 == 0:
                    half = (st.k // 2) % 2
                    if has_prior(st, 4):
                        wait_alone(sp, F["out_ps"], st.t - 2)
                    sp.dma_start(W1s[half][:], w1[st.pair]).then_inc(w_in[half], 16)
                    sp.dma_start(W2s[half][:].rearrange("p (f d) -> p f d", f=FB), w2[st.pair])\
                        .then_inc(w_in[half], 16)

            def store_experts(st):
                if has_prior(st, 2):
                    wait_alone(sp, eo_stored[st.k % 2], 16 * st.pair)
                wait_alone(sp, F["eo"], st.t + 1)
                sp.dma_start(eo_rows[:, bass.ts(st.t, G), :], eo[st.k % 2][:])\
                    .then_inc(eo_stored[st.k % 2], 16)

            def load_first_x1(st):
                if not st.steady and st.t >= NG - 4:
                    i = st.t - (NG - 4)
                    sp.dma_start(x2[i][:], X[:, i * TPB:(i + 1) * TPB, :]).then_inc(x1_in[i], 16)

            run_slots(sp, NG, 4, [(load_weights, 0), (load_first_x1, 4), (store_experts, 4)])

            def load_x1(st):
                if st.steady or st.t >= 4:
                    wait_alone(sp, C["out_ps"], st.t - 3)
                    sp.wait_ge(C["out0_ps"], st.t - 3)
                    sp.dma_start(x2[st.k][:], X[:, bass.ts(st.t, TPB), :]).then_inc(x1_in[st.k], 16)

            def store_out(st):
                if has_prior(st, 2):
                    wait_alone(sp, out_stored[st.k % 2], 16 * st.pair)
                wait_alone(sp, C["fin"], st.t + 1)
                sp.dma_start(out[:, bass.ts(st.t, TPB), :], fin[st.k % 2][:])\
                    .then_inc(out_stored[st.k % 2], 16)

            run_slots(sp, B, 4, [(load_x1, 0), (store_out, 8)])
            for s in out_stored:
                sp.wait_ge(s, 16 * B // 2)

        @block.gpsimd
        def _(pool):
            pool.memset(ident[:], 0.0).then_inc(consts_made, 1)
            pool.memset(block_mask[:], 1.0).then_inc(consts_made, 1)
            pool.memset(before[:], 0.0).then_inc(consts_made, 1)
            pool.memset(ones[:], 1.0).then_inc(consts_made, 1)
            pool.memset(ONEf[:], 1.0).then_inc(consts_made, 1)
            pool.memset(neg_half[:], -0.5).then_inc(consts_made, 1)
            for v in vt:
                pool.memset(v[:, :, D:D + 1], 1.0).then_inc(consts_made, 1)
            for y in y4T:
                pool.memset(y[:, 0:1], 0.0).then_inc(consts_made, 1)
            pool.iota(iota_e[:], [[-1, E]], base=E, channel_multiplier=0,
                      allow_small_or_imprecise_dtypes=True).then_inc(consts_made, 1)
            pool.iota(iota_lo[:], [[1, P]], base=0, channel_multiplier=0,
                      allow_small_or_imprecise_dtypes=True).then_inc(consts_made, 1)
            pool.iota(iota_tile[:], [[1, NT]], base=0, channel_multiplier=0,
                      allow_small_or_imprecise_dtypes=True).then_inc(consts_made, 1)
            pool.iota(iota_part[:], [[0, 1]], base=0, channel_multiplier=1,
                      allow_small_or_imprecise_dtypes=True).then_inc(consts_made, 1)
            pool.wait_ge(consts_made, 14)
            pool.affine_select(out=ident[:], in_=ident[:], compare_op=ALU.not_equal, fill=1.0, base=0,
                               pattern=[[-1, P]], channel_multiplier=1).then_inc(consts_made, 1)
            pool.affine_select(out=before[:], in_=before[:], compare_op=ALU.is_gt, fill=-1.0, base=0,
                               pattern=[[1, P]], channel_multiplier=-1).then_inc(consts_made, 1)
            by_head = block_mask[:, 0:D].rearrange("p (h j) -> p h j", j=HD)
            heads = block_mask[:, D:D + HEADS]
            pool.affine_select(out=by_head, in_=by_head, compare_op=ALU.is_ge, fill=0.0, base=0,
                               pattern=[[-HD, HEADS], [0, HD]], channel_multiplier=1).then_inc(consts_made, 1)
            pool.affine_select(out=heads, in_=heads, compare_op=ALU.is_ge, fill=0.0, base=0,
                               pattern=[[-HD, HEADS]], channel_multiplier=1).then_inc(consts_made, 1)
            pool.wait_ge(consts_made, 18)
            pool.affine_select(out=by_head, in_=by_head, compare_op=ALU.is_ge, fill=0.0, base=HD - 1,
                               pattern=[[HD, HEADS], [0, HD]], channel_multiplier=-1).then_inc(consts_made, 1)
            pool.affine_select(out=heads, in_=heads, compare_op=ALU.is_ge, fill=0.0, base=HD - 1,
                               pattern=[[HD, HEADS]], channel_multiplier=-1).then_inc(consts_made, 1)
            pool.wait_ge(consts_made, consts)

            def rsqrt(st, nb, norm, used, used_):
                i = st.k % 2
                wait_alone(pool, norm["mv"], st.t + 1)
                pool.tensor_scalar(nb["veps"][i][:], nb["mv"][i][:, :, 1], EPS, 1.0, ALU.add, ALU.mult)\
                    .then_inc(norm["veps"], 1)
                pool.tensor_scalar(nb["nmean"][i][:], nb["mv"][i][:, :, 0], -1.0, 1.0, ALU.mult, ALU.mult)\
                    .then_inc(norm["nmean"], 1)
                wait_alone(pool, norm["veps"], st.t + 1)
                if has_prior(st, 2):
                    pool.wait_ge(used[used_], st.t - 1)
                pool.tensor_tensor(nb["rstd"][i][:], nb["veps"][i][:], neg_half[:], ALU.pow)\
                    .then_inc(norm["rstd"], 1)
                wait_alone(pool, norm["rstd"], st.t + 1)
                pool.wait_ge(norm["nmean"], st.t + 1)
                pool.tensor_tensor(nb["nmr"][i][:], nb["nmean"][i][:], nb["rstd"][i][:], ALU.mult)\
                    .then_inc(norm["nmr"], 1)

            def rsqrt1(st):
                rsqrt(st, norm1, N1, S, "xn")

            def rsqrt2(st):
                rsqrt(st, norm2, N2, S, "xm")

            run_slots(pool, B, 2, [
                (rsqrt1, 0), (rsqrt2, 5)])

            for q in range(CH):
                cols, tiles = slice(q * CW, (q + 1) * CW), slice(q % (CH // K) * CW, (q % (CH // K) + 1) * CW)
                pool.wait_ge(hi_made, q + 1)
                pool.tensor_tensor(OHID[:, cols, 0:NS], OHHI[:, cols, :],
                                   iota_tile[:, tiles].unsqueeze(2).to_broadcast([P, CW, NS]), ALU.mult)\
                    .then_inc(by_tile, 1)

            pool.wait_ge(ids_ready, 1)
            for s in xn_stored:
                pool.wait_ge(s, 16 * B // 2)

            def gather_rows(st):
                i = st.k % 2
                if has_prior(st, 2):
                    wait_alone(pool, F["xgT_ps"], st.t - 1)
                    pool.wait_ge(xg_in[i], 16 * G * st.pair)
                pool.tensor_copy(SIDX_col[i][:], SIDX[:, bass.ts(st.t, G)]).then_inc(F["idx"], 1)
                wait_alone(pool, F["idx"], st.t + 1)
                for j in range(G):
                    pool.indirect_dma_start(
                        xg[i][:, j, :], None, xn_dram,
                        bass.IndirectOffsetOnAxis(ap=SIDX_col[i][:, j:j + 1], axis=0)).then_inc(xg_in[i], 16)

            run_slots(pool, NG, 4, [(gather_rows, 0)])
            for s in eo_stored:
                pool.wait_ge(s, 16 * NG // 2)

            def gather_first(st):
                i, i4 = st.k % 2, st.k
                pool.tensor_copy(EIDX_col[i4][:], EIDX[:, bass.ts(st.t, TPB * K)]).then_inc(C["idx"], 1)
                wait_alone(pool, C["idx"], st.t + 1)
                wait_alone(pool, x1_in[i4], 16 * (st.quad + 1))
                for n in range(TPB):
                    pool.indirect_dma_start(
                        x2[i4][:, n, :], None, eo_dram,
                        bass.IndirectOffsetOnAxis(ap=EIDX_col[i4][:, K * n:K * n + 1], axis=0),
                        compute_op=ALU.add).then_inc(e0_in[i], 16)

            def gather_second(st):
                i, i4 = st.k % 2, st.k
                wait_alone(pool, e0_in[i], 16 * TPB * (st.pair + 1))
                for n in range(TPB):
                    pool.indirect_dma_start(
                        x2[i4][:, n, :], None, eo_dram,
                        bass.IndirectOffsetOnAxis(ap=EIDX_col[i4][:, K * n + 1:K * n + 2], axis=0),
                        compute_op=ALU.add).then_inc(e1_in[i], 16)

            def products_kv(st):
                wait_alone(pool, C["qke"], st.t + 1)
                if has_prior(st, 2):
                    pool.wait_ge(C["tv_ps"], st.t - 1)
                pool.tensor_tensor(*outer_kv(st.k % 2, 1), ALU.mult).then_inc(C["p1_pool"], 1)

            def rsqrt_squares(st, nb, norm, used, used_):
                i = st.k % 2
                wait_alone(pool, norm["veps"], st.t + 1)
                if has_prior(st, 2):
                    pool.wait_ge(used[used_], st.t - 1)
                pool.tensor_tensor(nb["rstd"][i][:], nb["veps"][i][:], neg_half[:], ALU.pow)\
                    .then_inc(norm["rstd"], 1)
                wait_alone(pool, norm["rstd"], st.t + 1)
                pool.tensor_tensor(nb["nmr"][i][:], nb["nmean"][i][:], nb["rstd"][i][:], ALU.mult)\
                    .then_inc(norm["nmr"], 1)

            def rsqrt3(st):
                rsqrt_squares(st, norm1, N3, C, "y3")

            def rsqrt4(st):
                rsqrt_squares(st, norm2, N4, C, "y4")

            def finish(st):
                i = st.k % 2
                if has_prior(st, 2):
                    wait_alone(pool, out_stored[i], 16 * st.pair)
                wait_alone(pool, C["rkv"], st.t + 1)
                pool.tensor_tensor(fin[i][:], rkv[i][:], x3[st.k][:], ALU.add).then_inc(C["fin"], 1)

            run_slots(pool, B, 4, [
                (rsqrt4, 4), (gather_first, 0), (rsqrt3, 1), (products_kv, 2),
                (gather_second, 0), (finish, 6)])

        @block.scalar
        def _(act):
            def evacuate(st, sems, ready, done, dst, src):
                act.wait_ge(sems[ready], st.t + 1)
                act.activation(dst, src, ACT.Copy).then_inc(sems[done], 1)

            def normalize(st, norm, nb, sems, done, dst, rows):
                i = st.k % 2
                for n in range(TPB):
                    act.activation(dst[i][:, n, :], rows(n), ACT.Identity, scale=nb["rstd"][i][:, n:n + 1],
                                   bias=nb["nmr"][i][:, n:n + 1])\
                        .then_inc(sems[done + "0" * (n == 0)], 1)

            def tiles(ps):
                return ps[:, 0:TPB * D].rearrange("p (n d) -> p n d", n=TPB)

            def apply1(st):
                wait_alone(act, N1["nmr"], st.t + 1)
                if has_prior(st, 2):
                    act.wait_ge(S["xnT_ps"], st.t - 1)
                normalize(st, N1, norm1, S, "xn", xn, lambda n: X[:, st.t * TPB + n, :])

            def evac_xn(st):
                evacuate(st, S, "xnT_ps", "xnT", xnT[st.k % 2][:], bank[0][:, 0:T])

            def evac_xm(st):
                evacuate(st, S, "xmT_ps", "xmT", xmT[st.k % 2][:], bank[7][:, 0:T])

            def evac_att(st):
                evacuate(st, S, "attT_ps", "attT", attT[st.k % 2][:], bank[5][:, 0:T])

            def exps(st):
                i = st.k % 2
                act.wait_ge(S["proj"], st.t + 1)
                if has_prior(st, 2):
                    act.wait_ge(S["em"], st.t - 1)
                    act.wait_ge(S["kv_ps"], st.t - 1)
                kvp = bank[2].rearrange("p (n w d) -> p n w d", n=TPB, w=2)
                act.activation(eq[i][:, 0:T], bank[1][:, 0:T], ACT.Exp).then_inc(S["eq0"], 1)
                act.activation(eq[i][:, T:].rearrange("p (n d) -> p n d", n=TPB), kvp[:, :, 0, :],
                               ACT.Exp).then_inc(S["eq"], 1)
                act.activation(vt[i][:, :, 0:D], kvp[:, :, 1, :], ACT.Copy).then_inc(S["v"], 1)

            def apply2(st):
                wait_alone(act, S["x1"], st.t + 1)
                act.wait_ge(N2["nmr"], st.t + 1)
                if has_prior(st, 2):
                    act.wait_ge(S["xmT_ps"], st.t - 1)
                    act.wait_ge(xn_stored[st.k % 2], 16 * st.pair)
                normalize(st, N2, norm2, S, "xm", xm, lambda n: X[:, st.t * TPB + n, :])

            def keep_logits(st):
                wait_alone(act, S["logits"], st.t + 1)
                act.activation(LG[:, :, bass.ts(st.t, TPB)],
                               bank[7][:, T:T + TPB * E].rearrange("p (n e) -> p e n", n=TPB), ACT.Copy)\
                    .then_inc(S["lg"], 1)

            run_slots(act, B, 2, [
                (evac_att, 4), (evac_xn, 1), (apply1, 0), (evac_xm, 6),
                (apply2, 5), (exps, 1), (keep_logits, 6)])

            act.wait_ge(gates_diff, 1)
            act.activation(GE[:], GD[:], ACT.Exp).then_inc(gates_exp, 1)
            for q in range(CH):
                cols = slice(q * CW, (q + 1) * CW)
                act.wait_ge(hi_made, q + 1)
                act.activation(OHID[:, cols, NS:], OHHI[:, cols, :], ACT.Copy, scale=iota_part[:, 0:1])\
                    .then_inc(by_part, 1)

            def split_weights(st):
                if st.k % 2 == 0:
                    half = (st.k // 2) % 2
                    act.wait_ge(w_in[half], 32 * (st.quad + 1))
                    if has_prior(st, 4):
                        act.wait_ge(F["h_ps"], FB * (st.t - 2))
                    act.activation(W1hi[half][:], W1s[half][:], ACT.Copy).then_inc(F["whi"], 1)

            def split_x(st):
                i = st.k % 2
                act.wait_ge(F["xgT_ps"], st.t + 1)
                if has_prior(st, 2):
                    act.wait_ge(F["h_ps"], FB * st.t - FB)
                act.activation(xhi[i][:], bank[i], ACT.Copy).then_inc(F["xhi"], 1)

            def gelu(st):
                for f in range(FB):
                    act.wait_ge(F["h_ps"], FB * st.t + f + 1)
                    if f == 0 and has_prior(st, 2):
                        act.wait_ge(F["out_ps"], st.t - 1)
                    act.activation(h[st.k % 2][:, f, :], bank[2 + f], ACT.Gelu).then_inc(F["h"], 1)

            run_slots(act, NG, 4, [
                (split_weights, 0), (split_x, 0), (gelu, 1)])

            def center(st, nb, norm, sums_):
                i = st.k % 2
                act.wait_ge(norm["sum"], st.t + 1)
                if has_prior(st, 2):
                    act.wait_ge(norm["nmr"], st.t - 1)
                act.activation(nb["nmean"][i][:], sums_[i][:], ACT.Copy, scale=-1.0 / D).then_inc(norm["nmean"], 1)

            def squares(st, nb, norm, rows, scratch, square_sums):
                i = st.k % 2
                act.wait_ge(norm["nmean"], st.t + 1)
                for n in range(TPB):
                    act.activation(scratch[i][:, n, :], rows(n), ACT.Square, bias=nb["nmean"][i][:, n:n + 1],
                                   accum_out=square_sums[i][:, n:n + 1])\
                        .then_inc(norm["squares0" if n == 0 else "squares"], 1)

            def variance(st, nb, norm, square_sums):
                i = st.k % 2
                act.wait_ge(norm["squares"], st.t + 1)
                if has_prior(st, 2):
                    act.wait_ge(norm["rstd"], st.t - 1)
                act.activation(nb["veps"][i][:], square_sums[i][:], ACT.Copy, bias=EPS, scale=1.0 / D)\
                    .then_inc(norm["veps"], 1)

            def center3(st):
                center(st, norm1, N3, sum3)

            def center4(st):
                center(st, norm2, N4, sum4)

            def variance3(st):
                variance(st, norm1, N3, square_sum3)

            def variance4(st):
                variance(st, norm2, N4, square_sum4)

            def sum_x2(st):
                i = st.k % 2
                wait_alone(act, e1_in[i], 16 * TPB * (st.pair + 1))
                if has_prior(st, 2):
                    act.wait_ge(N3["nmean"], st.t - 1)
                for n in range(TPB):
                    act.activation(copy3[i][:, n, :], x2[st.k][:, n, :], ACT.Copy, accum_out=sum3[i][:, n:n + 1])\
                        .then_inc(N3["sum0" if n == 0 else "sum"], 1)

            def squares3(st):
                squares(st, norm1, N3, lambda n: x2[st.k][:, n, :], scratch3, square_sum3)

            def squares4(st):
                squares(st, norm2, N4, lambda n: x3[st.k][:, n, :], scratch4, square_sum4)

            def apply3(st):
                wait_alone(act, N3["nmr"], st.t + 1)
                if has_prior(st, 2):
                    act.wait_ge(C["y3T_ps"], st.t - 1)
                normalize(st, N3, norm1, C, "y3", y3, lambda n: x2[st.k][:, n, :])

            def evac_y3(st):
                evacuate(st, C, "y3T_ps", "y3T", y3T[st.k % 2][:], bank[0][:, 0:T])

            def keep_v(st):
                act.wait_ge(C["proj"], st.t + 1)
                if has_prior(st, 2):
                    act.wait_ge(C["p1"], st.t - 1)
                    act.wait_ge(C["p1_pool"], st.t - 1)
                act.activation(vc[st.k % 2][:], psum[:, 1:3, 2 * D:3 * D], ACT.Copy).then_inc(C["v"], 1)

            def exps_qk(st):
                i = st.k % 2
                if has_prior(st, 2):
                    act.wait_ge(C["p1"], st.t - 1)
                    act.wait_ge(C["rks"], st.t - 1)
                    act.wait_ge(C["qn"], st.t - 1)
                    act.wait_ge(C["p1_pool"], st.t - 1)
                act.wait_ge(C["qk"], st.t + 1)
                act.activation(qke[i][:], qk[i][:], ACT.Exp).then_inc(C["qke"], 1)

            def keep_x3(st):
                act.wait_ge(C["out0_ps"], st.t + 1)
                act.wait_ge(C["out_ps"], st.t + 1)
                if has_prior(st, 4):
                    act.wait_ge(C["fin"], st.t - 3)
                for n in range(TPB):
                    act.activation(x3[st.k][:, n, :], bank[4][:, n * D:(n + 1) * D], ACT.Copy,
                                   accum_out=sum4[st.k % 2][:, n:n + 1]).then_inc(N4["sum0" if n == 0 else "sum"], 1)

            def apply4(st):
                wait_alone(act, N4["sum"], st.t + 1)
                act.wait_ge(N4["nmr"], st.t + 1)
                if has_prior(st, 2):
                    act.wait_ge(C["y4T_ps"], st.t - 1)
                normalize(st, N4, norm2, C, "y4", y4, lambda n: x3[st.k][:, n, :])

            def evac_y4(st):
                evacuate(st, C, "y4T_ps", "y4T", y4T[st.k % 2][:, 1:], bank[5][:, 0:T])

            def gate_mix(st):
                i = st.k % 2
                act.wait_ge(C["rk_ps"], st.t + 1)
                act.activation(kr[i][:], bank[6][:, T:], ACT.Relu).then_inc(C["relu"], 1)
                if has_prior(st, 2):
                    act.wait_ge(C["rkv"], st.t - 1)
                act.activation(th[i][:], tiles(bank[6]), ACT.Tanh, scale=0.5).then_inc(C["th"], 1)
                act.wait_ge(C["relu"], st.t + 1)
                act.activation(ka[i][:], kr[i][:], ACT.Square).then_inc(C["ka"], 1)

            run_slots(act, B, 4, [
                (keep_x3, 3), (center4, 3), (squares4, 3), (variance4, 3),
                (keep_v, 1), (evac_y4, 4), (sum_x2, 0), (center3, 0), (squares3, 0), (variance3, 0), (exps_qk, 1), (apply4, 3), (apply3, 0), (gate_mix, 4), (evac_y3, 0)])

        @block.vector
        def _(dve):
            def norm_stats(st, norm, nb, rows):
                for n in range(TPB):
                    dve.bn_stats(nb["stats"][st.k % 2][:, n, :], rows(n)).then_inc(norm["stats"], 1)

            def norm_aggr(st, norm, nb):
                i = st.k % 2
                if has_prior(st, 2):
                    wait_alone(dve, norm["nmr"], st.t - 1)
                wait_alone(dve, norm["stats"], TPB * st.t + TPB)
                for n in range(TPB):
                    dve.bn_aggr(nb["mv"][i][:, n, :], nb["stats"][i][:, n, :])\
                        .then_inc(norm["aggr" if n == 0 else "mv"], 1)

            def mask_kv(st):
                i = st.k % 2
                dve.wait_ge(S["kv_ps"], st.t + 1)
                if has_prior(st, 2):
                    dve.wait_ge(S["num"], st.t - 1)
                dve.tensor_tensor(kv[i][:, 0:D], bank[3][:, 0:D], block_mask[:, 0:D], ALU.mult)\
                    .then_inc(S["kv0"], 1)
                dve.tensor_scalar(kv[i][:, D:], block_mask[:, D:], bank[3][:, D:D + 1], None, ALU.mult)\
                    .then_inc(S["kv"], 1)

            def stats_x(st):
                wait_alone(dve, x_in[st.k % 2], 16 * (st.pair + 1))
                norm_stats(st, N1, norm1, lambda n: X[:, st.t * TPB + n, :])

            def add_x1(st):
                rows = X[:, bass.ts(st.t, TPB), :]
                dve.wait_ge(S["wo"], st.t + 1)
                dve.tensor_tensor(rows, bank[6][:, 0:TPB * D].rearrange("p (n d) -> p n d", n=TPB), rows, ALU.add)\
                    .then_inc(S["x1"], 1)

            def stats_x1(st):
                wait_alone(dve, S["x1"], st.t + 1)
                norm_stats(st, N2, norm2, lambda n: X[:, st.t * TPB + n, :])

            def aggr_x(st):
                norm_aggr(st, N1, norm1)

            def aggr_x1(st):
                norm_aggr(st, N2, norm2)

            def divide(st):
                i = st.k % 2
                nd = bank[4][:, 0:TPB * (D + HEADS)].rearrange("p (n c) -> p n c", n=TPB)
                dve.wait_ge(S["num"], st.t + 1)
                dve.tensor_scalar(den[i][:], nd[:, :, D:], 1e-6, None, ALU.max).then_inc(S["den"], 1)
                dve.wait_ge(S["den"], st.t + 1)
                dve.reciprocal(rden[i][:], den[i][:]).then_inc(S["rden"], 1)
                dve.wait_ge(S["rden"], st.t + 1)
                if has_prior(st, 2):
                    dve.wait_ge(S["attT_ps"], st.t - 1)
                dve.tensor_tensor(
                    att[i][:].rearrange("p n (h j) -> p n h j", j=HD),
                    nd[:, :, 0:D].rearrange("p n (h j) -> p n h j", j=HD),
                    rden[i][:].unsqueeze(3).to_broadcast([P, TPB, HEADS, HD]), ALU.mult).then_inc(S["att"], 1)

            def clamp(st):
                i = st.k % 2
                dve.wait_ge(S["eq"], st.t + 1)
                dve.tensor_scalar(em[i][:], eq[i][:], 1.0, None, ALU.min).then_inc(S["em"], 1)

            def elu(st):
                i = st.k % 2
                dve.wait_ge(S["em"], st.t + 1)
                dve.wait_ge(S["v"], st.t + 1)
                if has_prior(st, 2):
                    dve.wait_ge(S["num"], st.t - 1)
                kvp = bank[2].rearrange("p (n w d) -> p n w d", n=TPB, w=2)
                dve.scalar_tensor_tensor(kt[i][:], kvp[:, :, 0, :], 1.0,
                                         em[i][:, T:].rearrange("p (n d) -> p n d", n=TPB),
                                         ALU.add, ALU.max).then_inc(S["elu0"], 1)
                dve.scalar_tensor_tensor(qT[i][:], bank[1][:, 0:T], 1.0, em[i][:, 0:T], ALU.add, ALU.max)\
                    .then_inc(S["elu"], 1)

            run_slots(dve, B, 2, [
                (elu, 4), (divide, 5), (add_x1, 6), (stats_x, 0),
                (stats_x1, 6), (aggr_x, 0), (mask_kv, 4), (aggr_x1, 6), (clamp, 3)])

            done = 0

            def chain(ins):
                nonlocal done
                done += 1
                ins.then_inc(routed, 1)
                dve.wait_ge(routed, done)

            def over_tiles(row):
                return row.unsqueeze(2).to_broadcast([P, E, NT])

            def over_experts(row):
                return row.unsqueeze(1).to_broadcast([P, E, NT])

            dve.wait_ge(S["lg"], B)
            left = LG
            for c in range(K):
                chain(dve.tensor_reduce(top[c][:], left[:].rearrange("p e t -> p t e"), AX.X, ALU.max))
                if c == 1:
                    dve.tensor_tensor(GD[:], top[1][:], top[0][:], ALU.subtract).then_inc(gates_diff, 1)
                chain(dve.tensor_tensor(hit[:], left[:], over_experts(top[c][:]), ALU.is_equal))
                chain(dve.tensor_tensor(numb[:], hit[:], over_tiles(iota_e[:]), ALU.mult))
                chain(dve.tensor_reduce(which[:], numb[:].rearrange("p e t -> p t e"), AX.X, ALU.max))
                chain(dve.tensor_tensor(OH[:, c], numb[:], over_experts(which[:]), ALU.is_equal))
                if c == 0:
                    chain(dve.scalar_tensor_tensor(lg[:], OH[:, 0], -3.0e38, LG[:], ALU.mult, ALU.add))
                    left = lg
            dve.tensor_tensor(CNT[:], OH[:, 0], OH[:, 1], ALU.add).then_inc(counts_made, 1)
            dve.wait_ge(counts_ps, 1)
            chain(dve.tensor_tensor_scan(CUM[:], ONEf[:], bank[1][:, 0:E * NT], 0.0, ALU.mult, ALU.add))
            chain(dve.tensor_tensor(BASE[:], bank[0][:, 0:E * NT], CUM[:], ALU.add))
            chain(dve.tensor_tensor(PRD[:].rearrange("p c e t -> p c (e t)"),
                                    OH[:].rearrange("p c e t -> p c (e t)"),
                                    BASE[:].unsqueeze(1).to_broadcast([P, K, E * NT]), ALU.mult))
            chain(dve.tensor_reduce(POSf[:], PRD[:].rearrange("p c e t -> p c t e"), AX.X, ALU.add))
            chain(dve.tensor_copy(POSu[:], POSf[:].rearrange("p c t -> p (c t)")))
            dve.tensor_scalar(HIu[:], POSu[:], P.bit_length() - 1, None, ALU.logical_shift_right)
            chain(dve.tensor_scalar(LOu[:], POSu[:], P - 1, None, ALU.bitwise_and))
            dve.tensor_copy(HIf[:], HIu[:])
            chain(dve.tensor_copy(LOf[:], LOu[:]))
            for q in range(CH):
                cols = slice(q * CW, (q + 1) * CW)
                dve.tensor_tensor(OHHI[:, cols, :], iota_lo[:, 0:NS].unsqueeze(1).to_broadcast([P, CW, NS]),
                                  HIf[:, cols].unsqueeze(2).to_broadcast([P, CW, NS]), ALU.is_equal)\
                    .then_inc(hi_made, 1)
                dve.tensor_tensor(OHLO[:, cols, :], iota_lo[:].unsqueeze(1).to_broadcast([P, CW, P]),
                                  LOf[:, cols].unsqueeze(2).to_broadcast([P, CW, P]), ALU.is_equal)\
                    .then_inc(lo_made, 1)
            by_choice = EIDX[:].rearrange("p (t c) -> p c t", c=K)
            dve.scalar_tensor_tensor(by_choice, LOf[:].rearrange("p (c t) -> p c t", c=K), float(NS),
                                     HIf[:].rearrange("p (c t) -> p c t", c=K), ALU.mult, ALU.add)\
                .then_inc(eidx_made, 1)
            dve.wait_ge(ids_ps, 1)
            chain(dve.tensor_copy(SIDXf[:], bank[2][:, 0:NS]))
            dve.scalar_tensor_tensor(SIDX[:], bank[2][:, NS:2 * NS], float(NT), SIDXf[:], ALU.mult, ALU.add)\
                .then_inc(ids_ready, 1)
            dve.wait_ge(gates_exp, 1)
            chain(dve.tensor_scalar(GS[:], GE[:], 1.0, None, ALU.add))
            chain(dve.reciprocal(GW[:, 0, :], GS[:]))
            chain(dve.tensor_tensor(GW[:, 1, :], GE[:], GW[:, 0, :], ALU.mult))
            gates = GW[:].rearrange("p c t -> p (c t)")
            for part in range(2):
                chain(dve.tensor_copy(gate_part[part][:], gates if part == 0 else gate_rest[:]))
                chain(dve.tensor_tensor(gate_rest[:], gates if part == 0 else gate_rest[:], gate_part[part][:],
                                        ALU.subtract))
            chain(dve.tensor_copy(gate_part[2][:], gate_rest[:]))

            def weigh_onehots(st):
                if st.steady or st.t >= len(GATE_CHUNKS):
                    return
                for q in GATE_CHUNKS[st.t]:
                    cols = slice(q * CW, (q + 1) * CW)
                    for part in range(3):
                        dve.tensor_tensor(OHW[:, cols, part * NS:(part + 1) * NS], OHHI[:, cols, :],
                                          gate_part[part][:, cols].unsqueeze(2).to_broadcast([P, CW, NS]),
                                          ALU.mult).then_inc(weighted, 1)

            def keep_gates(st):
                if not st.steady and st.t == 0:
                    dve.wait_ge(gates_ps, 1)
                    chain(dve.tensor_copy(gate_sum[:], bank[7][:, 2 * NS:3 * NS]))
                    chain(dve.tensor_tensor(gate_sum[:], bank[7][:, NS:2 * NS], gate_sum[:], ALU.add))
                    dve.tensor_tensor(WS[:], bank[7][:, 0:NS], gate_sum[:], ALU.add).then_inc(gates_ready, 1)
                    dve.wait_ge(gates_ready, 1)

            def rest_weights(st):
                if st.k % 2 == 0:
                    half = (st.k // 2) % 2
                    dve.wait_ge(F["whi"], st.pair + 1)
                    dve.tensor_tensor(W1lo[half][:], W1s[half][:], W1hi[half][:].bitcast(F32), ALU.subtract)\
                        .then_inc(F["wlo"], 1)

            def rest_x(st):
                i = st.k % 2
                dve.wait_ge(F["xhi"], st.t + 1)
                if has_prior(st, 2):
                    dve.wait_ge(F["h_ps"], FB * st.t - FB)
                dve.tensor_tensor(xlo[i][:], bank[i], xhi[i][:].bitcast(F32), ALU.subtract)\
                    .then_inc(F["xlo"], 1)

            def weigh_rows(st):
                i = st.k % 2
                dve.wait_ge(F["out_ps"], st.t + 1)
                if has_prior(st, 2):
                    dve.wait_ge(eo_stored[i], 16 * st.pair)
                dve.tensor_tensor(eo[i][:], bank[6 + i].rearrange("p (n d) -> p n d", n=G),
                                  WS[:, bass.ts(st.t, G)].unsqueeze(2).to_broadcast([P, G, D]), ALU.mult)\
                    .then_inc(F["eo"], 1)

            run_slots(dve, NG, 4, [
                (weigh_onehots, 0), (rest_weights, 0), (rest_x, 0), (keep_gates, 2),
                (weigh_rows, 2)])

            dve.tensor_scalar(OMM[:], MU[:], -1.0, 1.0, ALU.mult, ALU.add).then_inc(C["heads"], 1)
            dve.tensor_scalar(W[:, cFV:cFV + D], W[:, cFV:cFV + D], 0.5, None, ALU.mult).then_inc(C["heads"], 1)
            dve.wait_ge(C["heads"], 2)
            for j in range(2):
                dve.tensor_scalar(WP[:, j * D:(j + 1) * D], W[:, cFR + j * D:cFR + (j + 1) * D],
                                  OMM[:, j:j + 1], None, ALU.mult).then_inc(C["heads"], 1)
            for j in range(2):
                cols = W[:, cFR + j * D:cFR + (j + 1) * D]
                dve.tensor_scalar(cols, cols, MU[:, j:j + 1], None, ALU.mult).then_inc(C["heads"], 1)

            def maxima(st):
                i = st.k % 2
                dve.wait_ge(C["proj"], st.t + 1)
                dve.wait_ge(C["v"], st.t + 1)
                q_ = psum[:, 1:3, 0:D].rearrange("p n (h d) -> p n h d", d=HD)
                k_ = psum[:, 1:3, D:2 * D].rearrange("p n (h d) -> p n h d", d=HD)
                dve.tensor_reduce(qmax[i][:], q_, AX.X, ALU.max).then_inc(C["qmax"], 1)
                dve.tensor_reduce(kmax[i][:], k_.rearrange("p n h d -> p n d h"), AX.X, ALU.max)\
                    .then_inc(C["kmax"], 1)
                dve.wait_ge(C["qmax"], st.t + 1)
                if has_prior(st, 2):
                    dve.wait_ge(C["qke"], st.t - 1)
                dve.tensor_tensor(qk[i][:, :, 0:D].rearrange("p n (h d) -> p n h d", d=HD), q_,
                                  qmax[i][:].unsqueeze(3).to_broadcast([P, TPB, HEADS, HD]),
                                  ALU.subtract).then_inc(C["qk0"], 1)
                dve.wait_ge(C["kmax"], st.t + 1)
                dve.tensor_tensor(qk[i][:, :, D:].rearrange("p n (h d) -> p n h d", d=HD), k_,
                                  kmax[i][:].unsqueeze(2).to_broadcast([P, TPB, HEADS, HD]),
                                  ALU.subtract).then_inc(C["qk"], 1)

            def products_kv(st):
                dve.wait_ge(C["qke"], st.t + 1)
                if has_prior(st, 2):
                    dve.wait_ge(C["tv_ps"], st.t - 1)
                dve.tensor_tensor(*outer_kv(st.k % 2, 0), ALU.mult).then_inc(C["p1"], 1)

            def fold_heads(st):
                p = p1[st.k % 2]
                half = HEADS * HD * HD // 2
                dve.wait_ge(C["p1"], st.t + 1)
                dve.wait_ge(C["p1_pool"], st.t + 1)
                dve.tensor_tensor(p[:, :, 0:half], p[:, :, 0:half], p[:, :, half:], ALU.add)\
                    .then_inc(C["p1_sum"], 1)

            def sums(st):
                i = st.k % 2
                dve.wait_ge(C["qke"], st.t + 1)
                eq_ = qke[i][:, :, 0:D].rearrange("p n (h d) -> p n h d", d=HD)
                ek_ = qke[i][:, :, D:].rearrange("p n (h d) -> p n d h", d=HD)
                dve.tensor_reduce(qsum[i][:], eq_, AX.X, ALU.add).then_inc(C["qsum"], 1)
                dve.tensor_reduce(ksum[i][:], ek_, AX.X, ALU.add).then_inc(C["ksum"], 1)
                dve.wait_ge(C["qsum"], st.t + 1)
                dve.reciprocal(rqs[i][:], qsum[i][:]).then_inc(C["rqs"], 1)
                dve.wait_ge(C["ksum"], st.t + 1)
                dve.reciprocal(rks[i][:], ksum[i][:]).then_inc(C["rks"], 1)
                dve.wait_ge(C["rqs"], st.t + 1)
                dve.tensor_tensor(qn[i][:].rearrange("p n (h d) -> p n h d", d=HD), eq_,
                                  rqs[i][:].unsqueeze(3).to_broadcast([P, TPB, HEADS, HD]), ALU.mult)\
                    .then_inc(C["qn"], 1)

            def mean_v(st):
                i = st.k % 2
                if has_prior(st, 2):
                    dve.wait_ge(C["p2_0"], st.t - 1)
                    dve.wait_ge(C["p2"], st.t - 1)
                dve.wait_ge(C["rks"], st.t + 1)
                dve.wait_ge(C["tv_ps"], st.t + 1)
                dve.tensor_tensor(
                    tv[i][:].rearrange("p n (d e) -> p n d e", d=HD),
                    bank[3][:, 0:TPB * HD * HD].rearrange("p (n d e) -> p n d e", n=TPB, d=HD),
                    rks[i][:].unsqueeze(3).to_broadcast([P, TPB, HD, HD]), ALU.mult).then_inc(C["tv"], 1)

            def products_q(st, n):
                i = st.k % 2
                dve.wait_ge(C["tv"], st.t + 1)
                dve.wait_ge(C["qn"], st.t + 1)
                if has_prior(st, 1):
                    dve.wait_ge(C["out_ps" if n else "out0_ps"], st.t)
                dve.tensor_tensor(
                    p2[n][:].rearrange("p (d h e) -> p d h e", h=HEADS, d=HD),
                    qn[i][:, n, :].rearrange("p (h d) -> p d h", d=HD).unsqueeze(3)
                    .to_broadcast([P, HD, HEADS, HD]),
                    tv[i][:, n, :].rearrange("p (d e) -> p d e", d=HD).unsqueeze(2)
                    .to_broadcast([P, HD, HEADS, HD]), ALU.mult).then_inc(C["p2" if n else "p2_0"], 1)

            def products_q0(st):
                products_q(st, 0)

            def products_q1(st):
                products_q(st, 1)

            def fold_channels(st, n):
                w = FOLD[n] * D
                dve.wait_ge(C["p2" if n else "p2_0"], st.t + 1)
                dve.tensor_tensor(p2[n][:, 0:w], p2[n][:, 0:w], p2[n][:, HD * D - w:], ALU.add)\
                    .then_inc(C["p2_sum" if n else "p2_0_sum"], 1)

            def fold_channels0(st):
                fold_channels(st, 0)

            def fold_channels1(st):
                fold_channels(st, 1)

            def gate_values(st):
                i = st.k % 2
                dve.wait_ge(C["v_ps"], st.t + 1)
                if has_prior(st, 2):
                    dve.wait_ge(C["fin"], st.t - 1)
                dve.scalar_tensor_tensor(rkv[i][:], th[i][:], 1.0,
                                         bank[7][:, 0:TPB * D].rearrange("p (n d) -> p n d", n=TPB),
                                         ALU.add, ALU.mult).then_inc(C["rkv"], 1)

            run_slots(dve, B, 4, [
                (sums, 1), (maxima, 0), (mean_v, 1), (products_q1, 1),
                (fold_channels1, 1), (products_q0, 1), (fold_channels0, 1), (products_kv, 0), (fold_heads, 0), (gate_values, 4)])

        @block.tensor
        def _(pe):
            def transposes(st, sems, ready, done, dst, src):
                pe.wait_ge(sems[ready], st.t + 1)
                for n in range(TPB):
                    ins = pe.transpose(dst[:, n * P:(n + 1) * P], src(n), ident[:])
                ins.then_inc(sems[done], 1)

            pe.wait_ge(weights_in, 32)
            pe.wait_ge(consts_made, consts)

            def turn_xn(st):
                if has_prior(st, 1):
                    pe.wait_ge(S["xnT"], st.t)
                transposes(st, S, "xn", "xnT_ps", bank[0], lambda n: xn[st.k % 2][:, n, :])

            def sum_kv(st):
                i = st.k % 2
                pe.wait_ge(S["elu0"], st.t + 1)
                if has_prior(st, 1):
                    pe.wait_ge(S["kv"], st.t)
                for n in range(TPB):
                    ins = pe.matmul(bank[3][:, 0:D + 1], kt[i][:, n, :], vt[i][:, n, :],
                                    start=(n == 0), stop=(n == TPB - 1))
                ins.then_inc(S["kv_ps"], 1)

            def turn_xm(st):
                if has_prior(st, 1):
                    pe.wait_ge(S["lg"], st.t)
                transposes(st, S, "xm", "xmT_ps", bank[7], lambda n: xm[st.k % 2][:, n, :])

            def project(st):
                i = st.k % 2
                pe.wait_ge(S["xnT"], st.t + 1)
                if has_prior(st, 1):
                    pe.wait_ge(S["elu"], st.t)
                pe.matmul(bank[1][:, 0:T], W[:, cQ:cQ + D], xnT[i][:], start=True, stop=True)
                for n in range(TPB):
                    ins = pe.matmul(bank[2][:, 2 * D * n:2 * D * (n + 1)], xnT[i][:, n * P:(n + 1) * P],
                                    W[:, cKV:cKV + 2 * D], start=True, stop=True)
                ins.then_inc(S["proj"], 1)

            def project_out(st):
                i = st.k % 2
                pe.wait_ge(S["attT"], st.t + 1)
                if has_prior(st, 1):
                    pe.wait_ge(S["x1"], st.t)
                for n in range(TPB):
                    ins = pe.matmul(bank[6][:, n * D:(n + 1) * D], attT[i][:, n * P:(n + 1) * P],
                                    W[:, cO:cO + D], start=True, stop=True)
                ins.then_inc(S["wo"], 1)

            def attend(st):
                i = st.k % 2
                pe.wait_ge(S["kv"], st.t + 1)
                if has_prior(st, 1):
                    pe.wait_ge(S["att"], st.t)
                w = D + HEADS
                for n in range(TPB):
                    ins = pe.matmul(bank[4][:, n * w:(n + 1) * w], qT[i][:, n * P:(n + 1) * P], kv[i][:],
                                    start=True, stop=True)
                ins.then_inc(S["num"], 1)

            def route(st):
                i = st.k % 2
                pe.wait_ge(S["xmT"], st.t + 1)
                for n in range(TPB):
                    ins = pe.matmul(bank[7][:, T + n * E:T + (n + 1) * E], xmT[i][:, n * P:(n + 1) * P],
                                    W[:, cR:cR + E], start=True, stop=True)
                ins.then_inc(S["logits"], 1)

            def turn_att(st):
                if has_prior(st, 1):
                    pe.wait_ge(S["attT"], st.t)
                transposes(st, S, "att", "attT_ps", bank[5], lambda n: att[st.k % 2][:, n, :])

            run_slots(pe, B, 2, [
                (project_out, 4), (project, 1), (sum_kv, 2), (route, 6),
                (turn_att, 3), (turn_xn, 0), (attend, 2), (turn_xm, 5)])

            pe.wait_ge(counts_made, 1)
            cnt = CNT[:].rearrange("p e t -> p (e t)")
            pe.matmul(bank[1][:, 0:E * NT], ones[:], cnt, start=True, stop=True)
            pe.matmul(bank[0][:, 0:E * NT], before[:], cnt, start=True, stop=True).then_inc(counts_ps, 1)
            for j in range(K * NT):
                if j % CW == 0:
                    for made in (lo_made, by_tile, by_part):
                        pe.wait_ge(made, j // CW + 1)
                ins = pe.matmul(bank[2][:, 0:2 * NS], OHLO[:, j, :], OHID[:, j, :],
                                start=(j == 0), stop=(j == K * NT - 1))
            ins.then_inc(ids_ps, 1)

            def place_gates(st):
                if st.steady or st.t >= len(GATE_CHUNKS):
                    return
                for q in GATE_CHUNKS[st.t]:
                    pe.wait_ge(weighted, 3 * q + 3)
                    for j in range(q * CW, (q + 1) * CW):
                        ins = pe.matmul(bank[7][:, 0:3 * NS], OHLO[:, j, :], OHW[:, j, :],
                                        start=(j == 0), stop=(j == K * NT - 1))
                if q == CH - 1:
                    ins.then_inc(gates_ps, 1)

            def turn_rows(st):
                i = st.k % 2
                pe.wait_ge(xg_in[i], 16 * G * (st.pair + 1))
                if has_prior(st, 2):
                    pe.wait_ge(F["xlo"], st.t - 1)
                for n in range(G):
                    ins = pe.transpose(bank[i][:, n * P:(n + 1) * P], xg[i][:, n, :], ident[:])
                ins.then_inc(F["xgT_ps"], 1)

            def hidden(st):
                i, half = st.k % 2, (st.k // 2) % 2
                pe.wait_ge(F["xlo"], st.t + 1)
                if st.k % 2 == 0:
                    pe.wait_ge(F["wlo"], st.pair + 1)
                for f in range(FB):
                    if has_prior(st, 1):
                        pe.wait_ge(F["h"], FB * st.t - FB + f + 1)
                    hi, lo = (w[half][:, f * P:(f + 1) * P] for w in (W1hi, W1lo))
                    pe.matmul(bank[2 + f], hi, xhi[i][:], start=True, stop=False)
                    pe.matmul(bank[2 + f], hi, xlo[i][:], start=False, stop=False)
                    pe.matmul(bank[2 + f], lo, xhi[i][:], start=False, stop=True).then_inc(F["h_ps"], 1)

            def expert_rows(st):
                i, half = st.k % 2, (st.k // 2) % 2
                pe.wait_ge(F["h"], FB * st.t + FB)
                if has_prior(st, 2):
                    pe.wait_ge(F["eo"], st.t - 1)
                elif st.t == 1:
                    pe.wait_ge(gates_ready, 1)
                for n in range(G):
                    for f in range(FB):
                        ins = pe.matmul(bank[6 + i][:, n * D:(n + 1) * D], h[i][:, f, n * P:(n + 1) * P],
                                        W2s[half][:, f * D:(f + 1) * D], start=(f == 0), stop=(f == FB - 1))
                ins.then_inc(F["out_ps"], 1)

            run_slots(pe, NG, 4, [
                (turn_rows, 0), (place_gates, 0), (hidden, 1), (expert_rows, 2)])

            pe.wait_ge(C["heads"], 6)
            pe.wait_ge(F["eo"], NG)

            def turn_y3(st):
                if has_prior(st, 1):
                    pe.wait_ge(C["y3T"], st.t)
                transposes(st, C, "y3", "y3T_ps", bank[0], lambda n: y3[st.k % 2][:, n, :])

            def project_qkv(st):
                i = st.k % 2
                pe.wait_ge(C["y3T"], st.t + 1)
                if has_prior(st, 1):
                    pe.wait_ge(C["qk"], st.t)
                for n in range(TPB):
                    ins = pe.matmul(bank[1 + n][:, 0:3 * D], y3T[i][:, n * P:(n + 1) * P],
                                    W[:, cQKV:cQKV + 3 * D], start=True, stop=True)
                ins.then_inc(C["proj"], 1)

            def sum_heads(st):
                i = st.k % 2
                pe.wait_ge(C["p1_sum"], st.t + 1)
                if has_prior(st, 1):
                    pe.wait_ge(C["tv"], st.t)
                w = HD * HD
                for c in range(HEADS // 2):
                    ins = pe.matmul(bank[3][:, 0:TPB * w].rearrange("p (n w) -> p n w", n=TPB), ident[:],
                                    p1[i][:, :, c * w:(c + 1) * w], start=(c == 0), stop=(c == HEADS // 2 - 1))
                ins.then_inc(C["tv_ps"], 1)

            def sum_channels(st, n):
                dst = bank[4][:, n * D:(n + 1) * D]
                if has_prior(st, 1):
                    pe.wait_ge(N4["sum"], st.t)
                chunks = HD - FOLD[n]
                pe.matmul(dst, ident[:], x2[st.k][:, n, :], start=True, stop=False)
                pe.wait_ge(C["p2_sum" if n else "p2_0_sum"], st.t + 1)
                for c in range(chunks):
                    ins = pe.matmul(dst, ident[:], p2[n][:, c * D:(c + 1) * D], start=False, stop=(c == chunks - 1))
                ins.then_inc(C["out_ps" if n else "out0_ps"], 1)

            def sum_channels0(st):
                sum_channels(st, 0)

            def sum_channels1(st):
                sum_channels(st, 1)

            def turn_y4(st):
                if has_prior(st, 1):
                    pe.wait_ge(C["y4T"], st.t)
                transposes(st, C, "y4", "y4T_ps", bank[5], lambda n: y4[st.k % 2][:, n, :])

            def mix_rk(st):
                i = st.k % 2
                pe.wait_ge(C["y4T"], st.t + 1)
                if has_prior(st, 1):
                    pe.wait_ge(C["ka"], st.t)
                pe.matmul(bank[6][:, T:], W[:, cFK:cFK + D], y4T[i][:, 1:], start=True, stop=False)
                pe.matmul(bank[6][:, T:], WP[:, D:2 * D], y4T[i][:, 0:T], start=False, stop=True)
                for n in range(TPB):
                    dst = bank[6][:, n * D:(n + 1) * D]
                    pe.matmul(dst, y4T[i][:, 1 + n * P:1 + (n + 1) * P], W[:, cFR:cFR + D],
                              start=True, stop=False)
                    ins = pe.matmul(dst, y4T[i][:, n * P:(n + 1) * P], WP[:, 0:D], start=False, stop=True)
                ins.then_inc(C["rk_ps"], 1)

            def mix_values(st):
                i = st.k % 2
                pe.wait_ge(C["ka"], st.t + 1)
                if has_prior(st, 1):
                    pe.wait_ge(C["rkv"], st.t)
                for n in range(TPB):
                    ins = pe.matmul(bank[7][:, n * D:(n + 1) * D], ka[i][:, n * P:(n + 1) * P],
                                    W[:, cFV:cFV + D], start=True, stop=True)
                ins.then_inc(C["v_ps"], 1)

            run_slots(pe, B, 4, [
                (sum_channels1, 2), (turn_y3, 0), (sum_channels0, 2), (project_qkv, 0),
                (turn_y4, 3), (sum_heads, 1), (mix_rk, 3), (mix_values, 4)])


def kernel(**inputs):
    import numpy as np
    import concourse.bacc as bacc
    from concourse.bass_utils import run_bass_kernel_spmd

    x = np.asarray(inputs["L0_attn_x"])
    tiles = x.shape[0] * x.shape[1] // P

    def t(name):
        return np.asarray(inputs[name]).T

    arrays = {
        "x": np.ascontiguousarray(x.reshape(tiles, P, D).transpose(1, 0, 2)),
        "wa": np.ascontiguousarray(np.concatenate(
            [t("L0_attn_w_qkv"), t("L0_attn_w_out"), t("L0_ffn_Wr"), t("L1_attn_W_Q"), t("L1_attn_W_K"),
             t("L1_attn_W_V"), t("L1_ffn_W_r"), t("L1_ffn_W_k"), t("L1_ffn_W_v")], axis=1)),
        "w1": np.ascontiguousarray(inputs["L0_ffn_W1"]),
        "w2": np.ascontiguousarray(np.asarray(inputs["L0_ffn_W2"]).reshape(8, 4, P, D).transpose(0, 2, 1, 3)),
        "mu": np.ascontiguousarray(np.stack([inputs["L1_ffn_mu_r"], inputs["L1_ffn_mu_k"]], axis=1)),
    }
    nc = bacc.Bacc("TRN2", target_bir_lowering=False, num_devices=1)
    args = [nc.dram_tensor(name, a.shape, F32, kind="ExternalInput").ap() for name, a in arrays.items()]
    out = nc.dram_tensor("out", (P, tiles, D), F32, kind="ExternalOutput").ap()
    build(nc, *args, out)
    r = run_bass_kernel_spmd(nc, [arrays], core_ids=[0])
    return r.results[0]["out"].transpose(1, 0, 2).reshape(x.shape)
```
